# Optimizing a Trainium2 kernel written in Bass

```python
import numpy as np
import jax
import jax.numpy as jnp

def _softmax(x, axis=-1):
    return jax.nn.softmax(x, axis=axis)

def _gelu(x):
    return jax.nn.gelu(x, approximate=True)

def _silu(x):
    return jax.nn.silu(x)

def _sigmoid(x):
    return jax.nn.sigmoid(x)

def _layernorm(x, axis=-1, eps=1e-05):
    m = jnp.mean(x, axis=axis, keepdims=True)
    v = jnp.var(x, axis=axis, keepdims=True)
    return (x - m) / jnp.sqrt(v + eps)

def _scatter_add(tgt, idx, src, axis=0):
    return tgt.at[idx].add(src)

def _segment_sum(src, seg, n):
    return jax.ops.segment_sum(src, seg, n)
kernel_name = 'mk_flamingo_gated_d2_seqx_r2_bdea9f'

def setup_inputs(seed: int=0):
    np.random.seed(seed)
    _w = jnp.asarray

    def _rec_inputs():
        import jax
        import jax.numpy as jnp
        _rk = jax.random.key(seed)
        x = -0.0002928 + 1 * jax.random.normal(jax.random.fold_in(_rk, 1), (2, 2048, 512), jnp.float32)
        _lenS = 2048 - jax.random.randint(jax.random.fold_in(_rk, 7), (2,), 0, max(1, 2048 // 4) + 1, jnp.int32)
        _lenS2 = 128 - jax.random.randint(jax.random.fold_in(_rk, 8), (2,), 0, max(1, 128 // 4) + 1, jnp.int32)
        _ctx_1024P = jax.random.normal(jax.random.fold_in(_rk, 11), (2, 16, 512), jnp.float32)
        _ctx_1024c = jax.random.dirichlet(jax.random.fold_in(_rk, 511), 0.3 * jnp.ones((16,), jnp.float32), (2, 128))
        _ctx_1024t = jnp.einsum('bsk,bkd->bsd', _ctx_1024c, _ctx_1024P)
        _ctx_1024t = _ctx_1024t * jax.lax.rsqrt(jnp.mean(jnp.square(_ctx_1024t)) + 1e-12) * 0.953939
        ctx_1024 = -0.000137203 + 0.999727 * (_ctx_1024t + 0.3 * jax.random.normal(jax.random.fold_in(_rk, 611), (2, 128, 512), jnp.float32))
        _g = jax.random.normal(jax.random.fold_in(_rk, 9001), (2, 2), jnp.float32)
        _g = jnp.sign(_g) * jnp.maximum(jnp.abs(_g), 1.0) + (_g == 0) * 1.0
        g_xattn = _g[0]
        g_ffn = _g[1]
        return (x, ctx_1024, g_xattn, g_ffn)
    x, ctx_1024, g_xattn, g_ffn = _rec_inputs()

    def _L0_xattn_setup():
        import jax, jax.numpy as jnp
        import numpy as np
        DIM = 512
        NHEADS = 8
        HEAD_DIM = DIM // NHEADS
        ROPE_BASE = 10000.0

        def _rope(t, positions):
            d = t.shape[-1]
            inv_freq = 1.0 / ROPE_BASE ** (jnp.arange(0, d, 2, dtype=jnp.float32) / d)
            freqs = positions[:, None].astype(jnp.float32) * inv_freq
            emb = jnp.concatenate([freqs, freqs], axis=-1)
            cos = jnp.cos(emb)[None, :, None, :].astype(t.dtype)
            sin = jnp.sin(emb)[None, :, None, :].astype(t.dtype)
            t1, t2 = jnp.split(t, 2, axis=-1)
            rot = jnp.concatenate([-t2, t1], axis=-1)
            return t * cos + rot * sin
        key = jax.random.key(seed)
        k1, k2, k3, k4, k5 = jax.random.split(key, 5)
        B, T, S = (2, 1024, 1500)
        w_std = 1.0 / np.sqrt(DIM)
        return {'x': jax.random.normal(k1, (B, T, DIM), dtype=jnp.float32), 'xmel': jax.random.normal(k2, (B, S, DIM), dtype=jnp.float32), 'Wq': jax.random.normal(k3, (DIM, DIM), dtype=jnp.float32) * w_std, 'Wkv': jax.random.normal(k4, (2 * DIM, DIM), dtype=jnp.float32) * w_std, 'Wout': jax.random.normal(k5, (DIM, DIM), dtype=jnp.float32) * w_std}
    _L0_xattn_all = _L0_xattn_setup()
    _L0_xattn_in = {k: v for k, v in _L0_xattn_all.items() if k in ('Wq', 'Wkv', 'Wout')}
    del _L0_xattn_all

    def _L0_ffn_setup():
        import jax, jax.numpy as jnp
        import numpy as np

        def _bitlinear(x, w_latent):
            scale = jax.lax.stop_gradient(jnp.clip(jnp.mean(jnp.abs(w_latent), axis=1, keepdims=True), 1e-05, None))
            tern = jnp.clip(jnp.round(w_latent / scale), -1.0, 1.0)
            w = w_latent + jax.lax.stop_gradient(tern - w_latent)
            return x @ (w * scale).T
        key = jax.random.key(seed)
        ks = jax.random.split(key, 6)
        dim, hidden, rank = (512, 2048, 16)
        B, S = (4, 2048)
        x = jax.random.normal(ks[0], (B, S, dim), dtype=jnp.float32)
        w_fc = 0.02 * jax.random.normal(ks[1], (hidden, dim), dtype=jnp.float32)
        w_proj = 0.02 * jax.random.normal(ks[2], (dim, hidden), dtype=jnp.float32)
        u = 0.02 * jax.random.normal(ks[3], (hidden, rank), dtype=jnp.float32)
        v = 0.02 * jax.random.normal(ks[4], (rank, dim), dtype=jnp.float32)
        fast_b = jax.random.normal(ks[5], (rank, rank), dtype=jnp.float32)
        gate = jnp.float32(0.05)
        return {'x': x, 'fast_b': fast_b, 'w_fc': w_fc, 'w_proj': w_proj, 'u': u, 'v': v, 'gate': gate}
    _L0_ffn_all = _L0_ffn_setup()
    _L0_ffn_in = {k: v for k, v in _L0_ffn_all.items() if k in ('fast_b', 'w_fc', 'w_proj', 'u', 'v', 'gate')}
    del _L0_ffn_all

    def _L1_xattn_setup():
        import jax, jax.numpy as jnp
        import numpy as np
        D1, D2, D3 = (512, 512, 512)
        key = jax.random.key(seed)
        k1, k2, kw, kb = jax.random.split(key, 4)
        x1 = jax.random.normal(k1, (8, 1024, D1), dtype=jnp.float32)
        x2 = jax.random.normal(k2, (8, 1024, D2), dtype=jnp.float32)
        bound = 1.0 / np.sqrt(D1 + D2)
        W = jax.random.uniform(kw, (D3, D1 + D2), minval=-bound, maxval=bound, dtype=jnp.float32)
        b = jax.random.uniform(kb, (D3,), minval=-bound, maxval=bound, dtype=jnp.float32)
        return {'x1': x1, 'x2': x2, 'W': W, 'b': b}
    _L1_xattn_all = _L1_xattn_setup()
    _L1_xattn_in = {k: v for k, v in _L1_xattn_all.items() if k in ('W', 'b')}
    del _L1_xattn_all

    def _L1_ffn_setup():
        import jax, jax.numpy as jnp
        import numpy as np
        EPS = 1e-05

        def rmsnorm(x):
            return x * jax.lax.rsqrt(jnp.mean(x * x, axis=-1, keepdims=True) + EPS)

        def act_quant(x):
            scale = 127.0 / jnp.clip(jnp.max(jnp.abs(x), axis=-1, keepdims=True), 1e-05)
            q = jnp.clip(jnp.round(x * scale), -128.0, 127.0) / scale
            return x + jax.lax.stop_gradient(q - x)

        def weight_quant(w):
            scale = 1.0 / jnp.clip(jnp.mean(jnp.abs(w)), 1e-05)
            q = jnp.clip(jnp.round(w * scale), -1.0, 1.0) / scale
            return w + jax.lax.stop_gradient(q - w)

        def bitlinear(x, w, b):
            xq = act_quant(rmsnorm(x))
            wq = weight_quant(w)
            return jnp.einsum('bsd,fd->bsf', xq, wq) + b
        key = jax.random.key(seed)
        k0, k1, k2 = jax.random.split(key, 3)
        B, S, D, F = (2, 4096, 512, 2048)
        x = jax.random.normal(k0, (B, S, D), dtype=jnp.float32)
        w1 = jax.random.normal(k1, (F, D), dtype=jnp.float32) * (1.0 / np.sqrt(D))
        b1 = jnp.zeros((F,), dtype=jnp.float32)
        w2 = jax.random.normal(k2, (D, F), dtype=jnp.float32) * (1.0 / np.sqrt(F))
        b2 = jnp.zeros((D,), dtype=jnp.float32)
        return {'x': x, 'w1': w1, 'b1': b1, 'w2': w2, 'b2': b2}
    _L1_ffn_all = _L1_ffn_setup()
    _L1_ffn_in = {k: v for k, v in _L1_ffn_all.items() if k in ('w1', 'b1', 'w2', 'b2')}
    del _L1_ffn_all
    return {'x': x, 'ctx_1024': ctx_1024, 'g_xattn': g_xattn, 'g_ffn': g_ffn, 'L0_xattn_Wq': _L0_xattn_in['Wq'], 'L0_xattn_Wkv': _L0_xattn_in['Wkv'], 'L0_xattn_Wout': _L0_xattn_in['Wout'], 'L0_ffn_fast_b': _L0_ffn_in['fast_b'], 'L0_ffn_w_fc': _L0_ffn_in['w_fc'], 'L0_ffn_w_proj': _L0_ffn_in['w_proj'], 'L0_ffn_u': _L0_ffn_in['u'], 'L0_ffn_v': _L0_ffn_in['v'], 'L0_ffn_gate': _L0_ffn_in['gate'], 'L1_xattn_W': _L1_xattn_in['W'], 'L1_xattn_b': _L1_xattn_in['b'], 'L1_ffn_w1': _L1_ffn_in['w1'], 'L1_ffn_b1': _L1_ffn_in['b1'], 'L1_ffn_w2': _L1_ffn_in['w2'], 'L1_ffn_b2': _L1_ffn_in['b2']}

def reference(x, ctx_1024, g_xattn, g_ffn, L0_xattn_Wq, L0_xattn_Wkv, L0_xattn_Wout, L0_ffn_fast_b, L0_ffn_w_fc, L0_ffn_w_proj, L0_ffn_u, L0_ffn_v, L0_ffn_gate, L1_xattn_W, L1_xattn_b, L1_ffn_w1, L1_ffn_b1, L1_ffn_w2, L1_ffn_b2):
    import jax
    import jax.numpy as jnp

    def _L0_xattn_ref(x, xmel, Wq, Wkv, Wout):
        import jax, jax.numpy as jnp
        import numpy as np
        DIM = 512
        NHEADS = 8
        HEAD_DIM = DIM // NHEADS
        ROPE_BASE = 10000.0

        def _rope(t, positions):
            d = t.shape[-1]
            inv_freq = 1.0 / ROPE_BASE ** (jnp.arange(0, d, 2, dtype=jnp.float32) / d)
            freqs = positions[:, None].astype(jnp.float32) * inv_freq
            emb = jnp.concatenate([freqs, freqs], axis=-1)
            cos = jnp.cos(emb)[None, :, None, :].astype(t.dtype)
            sin = jnp.sin(emb)[None, :, None, :].astype(t.dtype)
            t1, t2 = jnp.split(t, 2, axis=-1)
            rot = jnp.concatenate([-t2, t1], axis=-1)
            return t * cos + rot * sin
        B, T, C = x.shape
        S = xmel.shape[1]
        H, D = (NHEADS, C // NHEADS)
        q = (x @ Wq.T).reshape(B, T, H, D)
        kv = (xmel @ Wkv.T).reshape(B, S, 2, H, D)
        q = _rope(q, jnp.arange(T))
        k = _rope(kv[:, :, 0], jnp.arange(S))
        v = kv[:, :, 1]
        scale = (C // H) ** (-0.25)
        q = q * scale
        k = k * scale
        scores = jnp.einsum('bthd,bshd->bhts', q, k)
        attn = jax.nn.softmax(scores, axis=-1)
        out = jnp.einsum('bhts,bshd->bthd', attn, v)
        out = out.reshape(B, T, C)
        return out @ Wout.T

    def _L0_ffn_ref(x, fast_b, w_fc, w_proj, u, v, gate):
        import jax, jax.numpy as jnp
        import numpy as np

        def _bitlinear(x, w_latent):
            scale = jax.lax.stop_gradient(jnp.clip(jnp.mean(jnp.abs(w_latent), axis=1, keepdims=True), 1e-05, None))
            tern = jnp.clip(jnp.round(w_latent / scale), -1.0, 1.0)
            w = w_latent + jax.lax.stop_gradient(tern - w_latent)
            return x @ (w * scale).T
        h = _bitlinear(x, w_fc) + gate * (x @ v.T @ fast_b.T @ u.T)
        r = jnp.maximum(h, 0.0)
        return _bitlinear(r * r, w_proj)

    def _L1_xattn_ref(x1, x2, W, b):
        import jax, jax.numpy as jnp
        import numpy as np
        D1, D2, D3 = (512, 512, 512)
        d1 = x1.shape[-1]
        W1 = W[:, :d1]
        W2 = W[:, d1:]
        part1 = jnp.einsum('bld,ed->ble', x1, W1)
        part2 = jnp.einsum('bld,ed->be', x2, W2) / x2.shape[1]
        return part1 + part2[:, None, :] + b

    def _L1_ffn_ref(x, w1, b1, w2, b2):
        import jax, jax.numpy as jnp
        import numpy as np
        EPS = 1e-05

        def rmsnorm(x):
            return x * jax.lax.rsqrt(jnp.mean(x * x, axis=-1, keepdims=True) + EPS)

        def act_quant(x):
            scale = 127.0 / jnp.clip(jnp.max(jnp.abs(x), axis=-1, keepdims=True), 1e-05)
            q = jnp.clip(jnp.round(x * scale), -128.0, 127.0) / scale
            return x + jax.lax.stop_gradient(q - x)

        def weight_quant(w):
            scale = 1.0 / jnp.clip(jnp.mean(jnp.abs(w)), 1e-05)
            q = jnp.clip(jnp.round(w * scale), -1.0, 1.0) / scale
            return w + jax.lax.stop_gradient(q - w)

        def bitlinear(x, w, b):
            xq = act_quant(rmsnorm(x))
            wq = weight_quant(w)
            return jnp.einsum('bsd,fd->bsf', xq, wq) + b
        h = bitlinear(x, w1, b1)
        h = jax.nn.gelu(h, approximate=False)
        return bitlinear(h, w2, b2)
    x = x + jnp.tanh(g_xattn[0]) * _L0_xattn_ref(_layernorm(x, axis=-1), ctx_1024, L0_xattn_Wq, L0_xattn_Wkv, L0_xattn_Wout)
    x = x + jnp.tanh(g_ffn[0]) * _L0_ffn_ref(_layernorm(x, axis=-1), L0_ffn_fast_b, L0_ffn_w_fc, L0_ffn_w_proj, L0_ffn_u, L0_ffn_v, L0_ffn_gate)
    x = x + jnp.tanh(g_xattn[1]) * _L1_xattn_ref(_layernorm(x, axis=-1), ctx_1024, L1_xattn_W, L1_xattn_b)
    x = x + jnp.tanh(g_ffn[1]) * _L1_ffn_ref(_layernorm(x, axis=-1), L1_ffn_w1, L1_ffn_b1, L1_ffn_w2, L1_ffn_b2)
    return x

_drawn_inputs = setup_inputs


def setup_inputs(seed=0):
    import zlib

    import numpy as np

    out = dict(_drawn_inputs(seed))
    spreads = {'g_ffn': (-1.0, 0.6), 'L1_ffn_b1': (0.0, 0.8), 'L1_ffn_b2': (0.0, 0.8)}
    factors = {'L0_ffn_fast_b': 8.0, 'L0_ffn_u': 8.0, 'L0_ffn_v': 8.0, 'L1_xattn_b': 27.848}
    for name, (base, spread) in spreads.items():
        noise = np.random.default_rng([zlib.crc32(name.encode()), seed]).standard_normal(out[name].shape)
        drawn = base * np.exp(spread * noise) if base else spread * noise
        out[name] = jnp.asarray(drawn.astype(out[name].dtype))
    for name, factor in factors.items():
        out[name] = (out[name] * factor).astype(out[name].dtype)
    return out
```

```python
from contextlib import ExitStack

import numpy as np
import concourse.bass as bass
from concourse import mybir

F32, F16, BF16, F8 = mybir.dt.float32, mybir.dt.float16, mybir.dt.bfloat16, mybir.dt.float8e4
ACT = mybir.ActivationFunctionType
ALU = mybir.AluOpType
AX = mybir.AxisListType

P = 128
D = 512
KC = D // P
HID = 2048
FC = HID // P
HEADS, HD = 8, 64
HALF = HD // 2
S = 128
BATCH, SEQ = 2, 2048
G = 256
TILES = G // P
GROUPS = BATCH * SEQ // G
PER_BATCH = SEQ // G
RANK = 16
REP = P // RANK
SLOTS = 16
EPS = 1e-5
TOP = 64.0
RMAX = 250.0
MAGIC = 12582912.0
TINY = 1e-30
KSIZE = 2 * 2 * 2 * 512
KVSIZE = KSIZE + 2 * D
PIECE = 2048


def build(nc, x_d, ctxT_d, gx_d, gf_d, wqT_d, wkvT_d, woT_d, fb_d, wfc_d, wproj_d, uT_d, vT_d, gate_d,
          wxT_d, wcT_d, bx_d, w1_d, b1_d, w2_d, b2_d, rope_d, mask_d, kv_d, out_d):
    ctx = ExitStack()
    with ctx:
        def sb(name, shape, dt):
            return ctx.enter_context(nc.sbuf_tensor(name, shape, dt))

        def sem(name):
            return ctx.enter_context(nc.semaphore(name))

        wq = sb("wq", [P, 2, KC, D], F16)
        wo = sb("wo", [P, 2, KC, D], F16)
        wx = sb("wx", [P, 2, KC, D], F16)
        fcT = sb("fcT", [P, KC, HID], F8)
        pjT = sb("pjT", [P, FC, D], F8)
        w1T = sb("w1T", [P, KC, HID], F8)
        w2T = sb("w2T", [P, FC, D], F8)
        lowA = sb("lowA", [P, HID], BF16)
        vrep = sb("vrep", [P, 2, KC, P], F16)
        kv = sb("kv", [P, KVSIZE], F16)
        k_now = kv[:, 0:KSIZE].rearrange("p (s h t n) -> p s h t n", s=2, h=2, t=2)
        v_now = kv[:, KSIZE:KVSIZE].rearrange("p (s n) -> p s n", s=2)
        rope = sb("rope", [P, 3, G], F32)
        scbc = sb("scbc", [P, D], F32)
        cb = sb("cb", [P, BATCH, D], F32)
        cb_now = sb("cb_now", [P, D], F32)
        b1bc = sb("b1bc", [P, HID], F32)
        b2bc = sb("b2bc", [P, D], F32)
        ident = sb("ident", [P, P], F32)
        ident16 = sb("ident16", [P, P], F16)
        identb = sb("identb", [P, P], BF16)
        ones = sb("ones", [P, P], F32)
        nhalf = sb("nhalf", [P, 1], F32)
        xa = sb("xa", [P, TILES, D], F32)
        xb = sb("xb", [P, TILES, D], F32)
        r1 = sb("r1", [P, TILES, D], F32)
        r1b = sb("r1b", [P, TILES, D], F32)
        r2 = sb("r2", [P, TILES, D], F32)
        r3 = sb("r3", [P, TILES, D], F32)
        x3n = sb("x3n", [P, TILES, D], F32)
        q4 = sb("q4", [P, TILES, D], F16)
        pt = sb("pt", [P, 2, HEADS, G], F16)
        xT1 = pt[:, 0, :, :].rearrange("p (s k) n -> p s k n", s=2)
        xT2 = sb("xT2", [P, 2, KC, G], F16)
        xT3 = sb("xT3", [P, 2, KC, G], F16)
        q4T = sb("q4T", [P, KC, G], F16)
        qT = sb("qT", [P, 2, 2, 2, G], F16)
        ao = qT[:, :, :, :, :].rearrange("p s h t n -> p s (h t) n")
        e = sb("e", [P, 4, 512], F32)
        ropeu, ropew = e[:, 0:2, :], e[:, 2:4, :]
        xn2 = e[:, 0:2, :]
        tlow = sb("tlow", [P, G], BF16)
        tres = sb("tres", [P, G], F32)
        tb2 = sb("tb2", [P, G], BF16)
        hid = sb("hid", [P, 2, FC, G], F16)
        rl = sb("rl", [P, 2, 512], F32)
        sq = sb("sq", [P, 2, 512], F32)
        h = sb("h", [P, TILES, HID], F32)
        q5 = sb("q5", [P, HID], F16)
        hT = sb("hT", [P, FC, P], F16)
        st = sb("st", [P, 4, TILES, 6], F32)
        mv = sb("mv", [P, 4, TILES, 2], F32)
        ve = sb("ve", [P, 5, TILES], F32)
        rs = sb("rs", [P, 5, TILES], F32)
        nmx = sb("nmx", [P, 4, 4], F32)
        esum = sb("esum", [P, 4, 4], F32)
        einv = sb("einv", [P, 4, 4], F32)
        amax = sb("amax", [P, 2, TILES], F32)
        zmax = sb("zmax", [P, 2, TILES], F32)
        zinv = sb("zinv", [P, 2, TILES], F32)
        qsc = sb("qsc", [P, 2, TILES], F32)
        dqs = sb("dqs", [P, 2, TILES], F32)
        ssq = sb("ssq", [P, TILES], F32)
        scf = sb("scf", [P, FC], F32)
        scd = sb("scd", [P, KC], F32)
        rsf = sb("rsf", [P, FC], F32)
        gsf = sb("gsf", [P, FC], F32)
        thr = sb("thr", [P, FC + KC], F32)
        nthr = sb("nthr", [P, FC + KC], F32)
        wmax = sb("wmax", [P, 4], F32)
        wmaxa = sb("wmaxa", [P, 4], F32)
        winv = sb("winv", [P, 4], F32)
        kvmax = sb("kvmax", [P, 2], F32)
        kvmaxa = sb("kvmaxa", [P, 2], F32)
        kvinv = sb("kvinv", [P, 2], F32)
        bnd = sb("bnd", [P, FC], F32)
        bmax = sb("bmax", [P, 1], F32)
        bmaxa = sb("bmaxa", [P, 1], F32)
        rho = sb("rho", [P, 1], F32)
        irho = sb("irho", [P, 1], F32)
        tg = sb("tg", [P, 4], F32)
        graw = sb("graw", [P, 4], F32)
        gate = sb("gate", [P, 1], F32)
        sig = sb("sig", [P, 1], F32)
        kapo = sb("kapo", [P, 1], F32)
        kapx = sb("kapx", [P, 1], F32)
        wsum = sb("wsum", [P, 8], F32)
        wmean = sb("wmean", [P, 2], F32)
        aw2t = sb("aw2t", [P, 1], F32)
        thr1 = sb("thr1", [P, 2], F32)
        nthr1 = sb("nthr1", [P, 2], F32)
        mask = sb("mask", [P, 4], F32)
        csum = sb("csum", [P, KC, BATCH], F32)
        c1 = sb("c1", [P, 1], F32)
        pad = sb("pad", [P, 1], F32)

        ps = ctx.enter_context(nc.psum_tensor("ps", [P, 8, 512], F32))
        FFN0, ATT0, BACK0 = 0, 2, 5

        def att_bank(n):
            return ps[:, ATT0 + n % 3, :]

        def back_bank(n):
            return ps[:, BACK0 + n % 3, :]

        hid32 = hid[:, :, :, :].rearrange("p s c n -> p (s c n)").bitcast(F32)
        h32 = h[:, :, :].rearrange("p t n -> p (t n)")
        piece = [hid32[:, 0:PIECE], hid32[:, PIECE:2 * PIECE], h32[:, 0:PIECE], h32[:, PIECE:2 * PIECE]]
        wq32 = piece[0]
        wo32 = pjT[:, :, :].rearrange("p c n -> p (c n)").bitcast(F32)
        wkv32 = h32.rearrange("p (k n) -> p k n", k=KC)
        wx32 = w1T[:, :, :].rearrange("p k n -> p (k n)").bitcast(F32).rearrange("p (k n) -> p k n", k=KC)
        wc32 = w2T[:, :, :].rearrange("p k n -> p (k n)").bitcast(F32).rearrange("p (k n) -> p k n", k=KC)
        wx32_flat = wx32.rearrange("p k n -> p (k n)")
        waste = w2T[:, :, :].rearrange("p k n -> p (k n)").bitcast(BF16)[:, 0:PIECE]
        ctxT = r2[:, :, :].rearrange("p t n -> p (t n)").rearrange("p (k n) -> p k n", k=KC)
        csb = r1b[:, :, :].rearrange("p t n -> p (t n)").rearrange("p (b k n) -> p b k n", b=BATCH, k=KC)
        krot = x3n[:, :, :]
        ktmp = rl[:, :, :]
        k16 = sq[:, :, :].rearrange("p a n -> p (a n)").bitcast(F16).rearrange("p (s n) -> p s n", s=2)
        pos = [q5[:, :], hT[:, :, :].rearrange("p c n -> p (c n)")]
        neg = [xT3[:, :, :, :].rearrange("p s k n -> p (s k n)"), r3[:, :, :].rearrange("p t n -> p (t n)").bitcast(F16)]
        k_both = fcT[:, :, :].rearrange("p k n -> p (k n)").bitcast(F16)
        k_other = [k_both[:, s * KSIZE // 2:(s + 1) * KSIZE // 2] for s in range(2)]
        v_other = q4T[:, :, :].rearrange("p k n -> p (k n)").rearrange("p (s n) -> p s n", s=2)
        small = q4[:, :, :].rearrange("p t n -> p (t n)").bitcast(F32)
        vT_sb = small[:, 0:KC * RANK].rearrange("p (k r) -> p k r", k=KC)
        fb_sb = small[0:RANK, 256:256 + RANK]
        uT = b1bc[0:RANK, :]
        low = r2[:, 1, 0:FC * RANK].rearrange("p (c r) -> p c r", c=FC)
        lowres = r2[:, 1, 256:256 + FC * RANK].rearrange("p (c r) -> p c r", c=FC)
        lowF = x3n[:, :, :].rearrange("p t n -> p (t n)").bitcast(BF16)[:, 0:HID].rearrange("p (c a r) -> p c a r", c=FC, a=REP)
        diag = r2[:, 0, :]
        lowprod = ps[:, 7, 0:FC * RANK].rearrange("p (c r) -> p c r", c=FC)

        (d_ctx, d_wk, d_wv, d_kr, d_wq, d_wo, d_wx, d_wc, d_small, d_u, d_b1, c_const, c_id16, c_kps, c_vps, c_kru,
         c_krot, c_wmax, c_wmaxa, c_wscale, c_whi, c_wlo, c_vrep, c_kvmax, c_kvmaxa, c_kvinv, c_kap, c_khi, c_klo,
         c_kblk, c_kvsave, c_vhi, c_vlo, c_cs, c_csb, c_cps, c_cb, c_tanh, c_wchain, c_scf, c_scale, c_b2, c_rows, c_thr, c_pos, c_quant,
         c_tern, c_quantp, c_lowps, c_low, c_lowzero, c_lowF, c_lowt, c_lowact, c_bnd, c_bndmax, c_rho, c_rsf, c_scd,
         c_scps, c_sc, c_asum, c_asumps, c_mean, c_cbnow) = [sem(n) for n in (
            "d_ctx d_wk d_wv d_kr d_wq d_wo d_wx d_wc d_small d_u d_b1 c_const c_id16 c_kps c_vps c_kru c_krot "
            "c_wmax c_wmaxa c_wscale c_whi c_wlo c_vrep c_kvmax c_kvmaxa c_kvinv c_kap c_khi c_klo c_kblk "
            "c_kvsave c_vhi c_vlo c_cs c_csb c_cps c_cb c_tanh c_wchain c_scf c_scale c_b2 c_rows c_thr c_pos c_quant c_tern c_quantp "
            "c_lowps c_low c_lowzero c_lowF c_lowt c_lowact c_bnd c_bndmax c_rho c_rsf c_scd c_scps c_sc c_asum "
            "c_asumps c_mean c_cbnow").split()]
        d_piece = [sem(f"d_piece{n}") for n in range(4)]
        xa_in, xb_in, rope_in, kv_in, r1_copied = [sem(n) for n in "xa_in xb_in rope_in kv_in r1_copied".split()]
        out_stored = [sem(f"out_stored{t}") for t in range(TILES)]
        (ln1, rs1, xn1, t1_ps, x1hi, x1lo, q_ps, rot_mul, rot_sum, q_hi, q_lo, s_ps, s_max, s_sub, s_exp, s_sum, s_inv,
         s_norm, pt_ps, p_hi, p_lo, pv_ps, ao_hi, ao_lo, wo_ps, x1_done, ln2, rs2, xn2_done, t2_ps, x2hi, x2lo, low_ps,
         low_b, low_r, low_done) = [sem(n) for n in (
             "ln1 rs1 xn1 t1_ps x1hi x1lo q_ps rot_mul rot_sum q_hi q_lo s_ps s_max s_sub s_exp s_sum s_inv "
             "s_norm pt_ps p_hi p_lo pv_ps ao_hi ao_lo wo_ps x1_done ln2 rs2 xn2_done t2_ps x2hi x2lo low_ps "
             "low_b low_r low_done").split()]
        up_ps, relu, sq_done, hid_hi, hid_lo, down_ps, down_mul, x2_done = [sem(n) for n in (
            "up_ps relu sq_done hid_hi hid_lo down_ps down_mul x2_done").split()]
        (ln3, rs3, xn3, t3_ps, x3hi, x3lo, x2c, wx_ps, x3_done, ln4, rs4, z4, q4_done, t4_ps, q4T_done, x3b, w1_ps,
         h_done, gelu, sqsum, z5, rs5, q5_done, t5_ps, hT_done, w2_ps, out_done) = [sem(n) for n in (
             "ln3 rs3 xn3 t3_ps x3hi x3lo x2c wx_ps x3_done ln4 rs4 z4 q4_done t4_ps q4T_done x3b w1_ps "
             "h_done gelu sqsum z5 rs5 q5_done t5_ps hT_done w2_ps out_done").split()]

        def need(eng, s, per, g, k):
            if isinstance(g, int) and g < 0:
                return
            eng.wait_ge(s, g * per + (k + 1))

        PARTS = ((0, 0), (0, 1), (1, 0))
        S_UNITS = [(t, hg) for t in range(TILES) for hg in range(2)]
        QUANT = [("fc", i) for i in range(4)] + [("pj", i) for i in range(4)] + \
                [("w1", i) for i in range(4)] + [("w2", i) for i in range(4)]
        LOADS = QUANT[0:8] + [("s1", i) for i in range(4)] + [("s2", i) for i in range(4)] + QUANT[8:16]
        LOAD_OF = [LOADS.index(q) for q in QUANT]
        PLACE = [(1, 2, 3, 0)[n % 4] if n < 16 else 2 + n % 2 for n in range(len(LOADS))]

        def arrived(eng, n):
            eng.wait_ge(d_piece[PLACE[n]], 16 * PLACE[:n + 1].count(PLACE[n]))

        THR = [(0, s) for s in (0, 1, 2, 3, 5, 6, 7, 8)]
        POS = THR + [(1, s) for s in (0, 1, 3, 5, 7, 8, 10, 12)]
        SIGN = [(0, s + 2) for _, s in THR] + [(1, s) for s in (1, 2, 4, 6, 8, 9, 11, 13)]
        TERN = [(j, s + 1) for j, s in SIGN]
        EVAC = [(j, s + 2) for j, s in SIGN]
        ROWS = (4, 5, 6, 7)
        SUMS = (10, 11, 12, 12, 13, 13, 14, 14)

        SL_T1, SL_Q, SL_S, SL_PT, SL_PV, SL_WO, SL_T2, SL_LOW = 0, (1, 2), (4, 5), (7, 8), 10, 11, 13, 14
        SL_LN1 = 13
        SL_T3, SL_WX, SL_T4, SL_W1, SL_T5, SL_W2 = (1, 2), (3, 4), (5, 6), (7, 9), (11, 13), (13, 15)
        SL_X2 = (11, 15)

        def sign_parts(q):
            kind, i = QUANT[q]
            if kind == "fc":
                return [(c * D, (c + 1) * D, thr[:, 4 * i + c:4 * i + c + 1], nthr[:, 4 * i + c:4 * i + c + 1])
                        for c in range(KC)]
            if kind == "pj":
                return [(0, PIECE, thr[:, FC + i:FC + i + 1], nthr[:, FC + i:FC + i + 1])]
            w = ("w1", "w2").index(kind)
            return [(0, PIECE, thr1[:, w:w + 1], nthr1[:, w:w + 1])]

        def first(g):
            return isinstance(g, int) and g == 0

        def main_loop(eng, body, change_at=None, change=None):
            for j in range(3):
                body(j, j - 1 if j >= 1 else None, j - 2 if j >= 2 else None, j + 1)
            if change is None:
                with eng.Fori(3, GROUPS - 1) as i:
                    body(i, i - 1, i - 2, i + 1)
            else:
                with eng.Fori(3, change_at) as i:
                    body(i, i - 1, i - 2, i + 1)
                change()
                with eng.Fori(change_at, GROUPS - 1) as i:
                    body(i, i - 1, i - 2, i + 1)
            body(GROUPS - 1, GROUPS - 2, GROUPS - 3, None)
            body(None, GROUPS - 1, GROUPS - 2, None)
            body(None, None, GROUPS - 1, None)

        block = ctx.enter_context(nc.Block())

        @block.sync
        def _(sp):
            def tokens(d, g):
                if isinstance(g, int):
                    return d[g].rearrange("(t p) n -> p t n", p=P)
                return d[bass.ds(g, 1)].rearrange("o (t p) n -> p (o t) n", p=P)

            def table(g):
                if isinstance(g, int):
                    return rope_d[g]
                return rope_d[bass.ds(g, 1)].rearrange("o p a n -> p (o a) n")

            chunks = lambda d: d.rearrange("(k p) n -> p k n", p=P)
            as_k = lambda ap: ap.rearrange("p (k n) -> p k n", k=KC)

            def load(n):
                kind, i = LOADS[n]
                place = PLACE[n]
                if n in (1, 2):
                    sp.wait_ge(c_vps, BATCH)
                elif n == 3:
                    sp.wait_ge(c_wlo, 1)
                elif 4 <= n < 12:
                    sp.wait_ge(c_quant, n - 3)
                elif 12 <= n < 16:
                    sp.wait_ge(c_asum, n - 11)
                elif 16 <= n < 18:
                    sp.wait_ge(c_asum, n - 10)
                elif n >= 18:
                    sp.wait_ge(c_quant, n - 9)
                src = {"fc": wfc_d, "pj": wproj_d, "s1": w1_d, "w1": w1_d, "s2": w2_d, "w2": w2_d}[kind]
                if kind in ("pj", "s2", "w2"):
                    sp.dma_start(piece[place], src[i * P:(i + 1) * P, :]).then_inc(d_piece[place], 16)
                else:
                    sp.dma_start(as_k(piece[place]), src[i * D:(i + 1) * D, :].rearrange("(c p) n -> p c n", p=P))\
                        .then_inc(d_piece[place], 16)

            def next_xa(g):
                need(sp, t1_ps, TILES, g, 1)
                sp.dma_start(xa[:, :, :], tokens(x_d, g + 1)).then_inc(xa_in, 16)

            def next_rope(g):
                need(sp, rot_sum, 2, g, 1)
                sp.dma_start(rope[:, :, :], table(g + 1)).then_inc(rope_in, 16)

            def next_xb(g):
                need(sp, x1_done, TILES, g, 1)
                sp.dma_start(xb[:, :, :], tokens(x_d, g + 1)).then_inc(xb_in, 16)

            def keep_r1(ga, gf):
                need(sp, x1_done, TILES, ga, 1)
                if gf is not None:
                    need(sp, x2_done, TILES, gf, 1)
                sp.dma_start(r1b[:, :, :], r1[:, :, :]).then_inc(r1_copied, 16)

            def body(ga, gf, gb, more=True):
                if ga is not None and more:
                    next_xa(ga)
                    next_rope(ga)
                    next_xb(ga)
                if gb is not None:
                    for t in range(TILES):
                        need(sp, out_done, TILES, gb, t)
                        dst = out_d[gb, t * P:(t + 1) * P, :] if isinstance(gb, int) else \
                            out_d[bass.ds(gb, 1), t * P:(t + 1) * P, :].rearrange("o p n -> (o p) n")
                        sp.dma_start(dst, r3[:, t, :]).then_inc(out_stored[t], 16)
                if ga is not None:
                    keep_r1(ga, gf)

            sp.dma_start(ctxT, chunks(ctxT_d)).then_inc(d_ctx, 16)
            sp.dma_start(wkv32[:, :, 0:D], chunks(wkvT_d[:, 0:D])).then_inc(d_wk, 16)
            sp.dma_start(as_k(wq32), chunks(wqT_d)).then_inc(d_wq, 16)
            sp.dma_start(wkv32[:, :, D:2 * D], chunks(wkvT_d[:, D:2 * D])).then_inc(d_wv, 16)
            load(0)
            sp.dma_start(as_k(wo32), chunks(woT_d)).then_inc(d_wo, 16)
            sp.dma_start(wc32, chunks(wcT_d)).then_inc(d_wc, 16)
            sp.dma_start(xb[:, :, :], tokens(x_d, 0)).then_inc(xb_in, 16)
            sp.wait_ge(c_kru, 6)
            sp.dma_start(rope[:, :, :], table(0)).then_inc(rope_in, 16)
            for n in range(1, 4):
                load(n)
            sp.dma_start(wx32, chunks(wxT_d)).then_inc(d_wx, 16)
            next_xa(0)
            next_rope(0)
            for n in range(4, 10):
                load(n)
            sp.wait_ge(c_lowps, 1)
            sp.dma_start(b1bc[:, :], b1_d.partition_broadcast(P)).then_inc(d_b1, 16)
            sp.wait_ge(c_cb, 2)
            sp.dma_start(cb_now[:, :], cb[:, 0, :]).then_inc(c_cbnow, 16)
            for n in range(10, 16):
                load(n)
            next_xb(0)
            keep_r1(0, None)
            load(16)
            load(17)
            next_xa(1)
            next_rope(1)
            for n in range(18, 24):
                load(n)
            next_xb(1)
            keep_r1(1, 0)
            body(2, 1, 0)
            with sp.Fori(3, PER_BATCH - 1) as i:
                body(i, i - 1, i - 2)
            j = PER_BATCH - 1
            need(sp, pv_ps, 2, j, 1)
            sp.dma_start(kv[:, :], kv_d).then_inc(kv_in, 16)
            body(j, j - 1, j - 2)
            body(j + 1, j, j - 1)
            need(sp, x2c, TILES, j, 1)
            sp.dma_start(cb_now[:, :], cb[:, 1, :]).then_inc(c_cbnow, 16)
            body(j + 2, j + 1, j)
            with sp.Fori(PER_BATCH + 2, GROUPS - 1) as i:
                body(i, i - 1, i - 2)
            j = GROUPS - 1
            body(j, j - 1, j - 2, more=False)
            body(None, j, j - 1)
            body(None, None, j)
            for t in range(TILES):
                sp.wait_ge(out_stored[t], 16 * GROUPS)
            sp.wait_ge(c_kvsave, 48)

        @block.gpsimd
        def _(pool):
            RMAXOP = bass.bass_isa.ReduceOp.max
            pool.memset(ident[:, :], 0.0).then_inc(c_const, 1)
            pool.memset(ones[:, :], 1.0).then_inc(c_const, 1)
            pool.memset(nhalf[:, :], -0.5).then_inc(c_const, 1)
            pool.wait_ge(c_const, 3)
            pool.affine_select(out=ident[:, :], in_=ident[:, :], compare_op=ALU.not_equal, fill=1.0, base=0,
                               pattern=[[-1, P]], channel_multiplier=1).then_inc(c_const, 1)

            def rsqrt(n, ready, per, k, done, g, t):
                need(pool, ready, per, g, k)
                pool.tensor_tensor(rs[:, n, t:t + 1], ve[:, n, t:t + 1], nhalf[:, :], ALU.pow).then_inc(done, 1)

            def rot(g, hg):
                need(pool, rot_mul, 6, g, 3 * hg + 2)
                pool.tensor_tensor(ropeu[:, hg, :], ropeu[:, hg, :], ropew[:, hg, :], ALU.add).then_inc(rot_sum, 1)

            def norm(g, n):
                need(pool, s_inv, 4, g, n)
                view = e[:, n, :].rearrange("p (h s) -> p h s", h=4)
                pool.tensor_tensor(view, view, einv[:, n, :].unsqueeze(2).broadcast_to([P, 4, S]), ALU.mult)\
                    .then_inc(s_norm, 1)

            def add_cb(g, t):
                if first(g) and t == 0:
                    pool.wait_ge(c_cbnow, 16)
                need(pool, xn3, TILES, g, t)
                pool.tensor_tensor(r2[:, t, :], r2[:, t, :], cb_now[:, :], ALU.add).then_inc(x2c, 1)

            def add_b2(g, t):
                need(pool, z4, 6 * TILES, g, 6 * t)
                pool.tensor_tensor(r3[:, t, :], r3[:, t, :], b2bc[:, :], ALU.add).then_inc(x3b, 1)

            def ln1_rsqrt(g):
                for t in range(TILES):
                    rsqrt(0, ln1, 3 * TILES, 3 * t + 2, rs1, g, t)

            def rotate_k(hg):
                pool.wait_ge(c_kru, 3 * hg + 3)
                pool.tensor_tensor(krot[:, hg, :], krot[:, hg, :], ktmp[:, hg, :], ALU.add).then_inc(c_krot, 1)

            def largest(ready, count, done, dst, src):
                pool.wait_ge(ready, count)
                pool.partition_all_reduce(dst, src, P, RMAXOP).then_inc(done, 1)

            def signs_above(q):
                kind, i = QUANT[q]
                pool.wait_ge(c_thr, q + 1)
                if q >= 2:
                    pool.wait_ge(c_quant, q - 1)
                arrived(pool, LOAD_OF[q])
                src = piece[PLACE[LOAD_OF[q]]]
                for a, b, t, _ in sign_parts(q):
                    last = pool.tensor_scalar(pos[q % 2][:, a:b], src[:, a:b], t, None, ALU.is_gt)
                last.then_inc(c_pos, 1)

            def prepare_first():
                ln1_rsqrt(0)
                rotate_k(0)
                largest(c_wmax, 1, c_wmaxa, wmaxa[:, 0:1], wmax[:, 0:1])
                rotate_k(1)
                largest(c_kvmax, 2, c_kvmaxa, kvmaxa[:, :], kvmax[:, :])
                pool.wait_ge(c_cs, 2)
                for b in range(BATCH):
                    for k in range(KC):
                        last = pool.tensor_tensor(csb[:, b, k, :], ones[:, :], csum[:, k, b:b + 1].broadcast_to([P, P]),
                                                  ALU.mult)
                last.then_inc(c_csb, 1)

            def prepare(j, s):
                if (j, s) == (0, 0):
                    largest(c_wmax, 3, c_wmaxa, wmaxa[:, 1:3], wmax[:, 1:3])
                    pool.wait_ge(c_klo, 1)
                    pool.memset(lowF, 0.0).then_inc(c_lowzero, 1)
                if (j, s) == (0, 7):
                    largest(c_bnd, 4, c_bndmax, bmaxa[:, :], bmax[:, :])
                if (j, s) == (0, 9):
                    largest(c_wmax, 4, c_wmaxa, wmaxa[:, 3:4], wmax[:, 3:4])
                if (j, s) in POS:
                    signs_above(POS.index((j, s)))

            def body(ga, gf, gb, gn):
                for s in range(SLOTS):
                    if ga is not None:
                        if s in SL_Q:
                            rot(ga, SL_Q.index(s))
                        if s - 1 in SL_S:
                            for n in (2 * SL_S.index(s - 1), 2 * SL_S.index(s - 1) + 1):
                                norm(ga, n)
                        if s == SL_WO:
                            for t in range(TILES):
                                rsqrt(1, ln2, 3 * TILES, 3 * t + 2, rs2, ga, t)
                    if gf is not None and s in SL_X2:
                        rsqrt(2, ln3, 3 * TILES, 3 * SL_X2.index(s) + 2, rs3, gf, SL_X2.index(s))
                    if gn is not None and s == SL_LN1:
                        ln1_rsqrt(gn)
                    if gb is not None:
                        if s in SL_T3:
                            add_cb(gb, SL_T3.index(s))
                        if s in SL_WX:
                            t = SL_WX.index(s)
                            rsqrt(3, ln4, 3 * TILES, 3 * t + 2, rs4, gb, t)
                            add_b2(gb, t)
                        if s in (SL_W1[0] + 2, SL_W1[1] + 2):
                            t = (SL_W1[0] + 2, SL_W1[1] + 2).index(s)
                            rsqrt(4, z5, 6 * TILES, 6 * t + 1, rs5, gb, t)
                    if isinstance(ga, int) and ga < 2:
                        prepare(ga, s)

            def next_batch():
                pool.wait_ge(c_cbnow, 32)

            prepare_first()
            main_loop(pool, body, PER_BATCH + 2, next_batch)

        @block.scalar
        def _(act):
            act.dma_start(rope[:, :, :], rope_d[GROUPS]).then_inc(d_kr, 16)
            act.dma_start(xa[:, :, :], x_d[0].rearrange("(t p) n -> p t n", p=P)).then_inc(xa_in, 16)
            for dst, src in ((mask[:, :], mask_d), (vT_sb, vT_d.rearrange("(k p) r -> p k r", p=P)), (fb_sb, fb_d),
                             (graw[:, 0:2], gx_d.partition_broadcast(P)), (graw[:, 2:4], gf_d.partition_broadcast(P)),
                             (gate[:, :], gate_d.partition_broadcast(P)), (b2bc[:, :], b2_d.partition_broadcast(P)),
                             (cb_now[:, :], bx_d.partition_broadcast(P))):
                act.dma_start(dst, src).then_inc(d_small, 16)
            act.dma_start(uT, uT_d).then_inc(d_u, 16)

            def weight_hi(n, col, src, dst):
                act.wait_ge(c_wscale, n + 1)
                act.activation(dst[:, 0, :, :].rearrange("p k n -> p (k n)"), src, ACT.Copy, scale=winv[:, col:col + 1])\
                    .then_inc(c_whi, 1)

            def evac(q):
                kind, i = QUANT[q]
                if q == 0:
                    act.wait_ge(c_kvsave, 48)
                if q == 4:
                    act.wait_ge(c_wlo, 2)
                for a in range(2):
                    act.wait_ge(c_tern, 2 * q + a + 1)
                    src = ps[:, 5 + a, :].bitcast(F16)
                    if kind in ("fc", "w1"):
                        dst = (fcT if kind == "fc" else w1T)[:, 2 * a:2 * a + 2, i * D:(i + 1) * D]
                        src = src.rearrange("p (k n) -> p k n", k=2)
                    else:
                        dst = (pjT if kind == "pj" else w2T)[:, 8 * a:8 * a + 8, i * P:(i + 1) * P]
                        src = src.rearrange("p (c n) -> p c n", n=P)
                    act.activation(dst, src, ACT.Copy, scale=-1.0, saturate=False).then_inc(c_quantp, 1)

            def prepare_first():
                weight_hi(0, 0, wq32, wq)
                act.wait_ge(c_kvinv, 2)
                act.activation(k16[:, 0, :], krot.rearrange("p h n -> p (h n)"), ACT.Copy, scale=kvinv[:, 0:1])\
                    .then_inc(c_khi, 1)
                for b, dst in enumerate((v_now, v_other)):
                    act.activation(dst[:, 0, :], ps[:, b, :], ACT.Copy, scale=kvinv[:, 1:2]).then_inc(c_vhi, 1)

            def prepare(j, s):
                if (j, s) == (0, 0):
                    act.wait_ge(d_small, 128)
                    act.activation(tg[:, :], graw[:, :], ACT.Tanh).then_inc(c_tanh, 1)
                if (j, s) == (0, 2):
                    weight_hi(1, 1, wo32, wo)
                    act.wait_ge(c_kblk, 2)
                    act.wait_ge(c_vlo, 2)
                    for a in range(2):
                        act.dma_start(kv_d[:, a * KSIZE // 2:(a + 1) * KSIZE // 2], k_other[a]).then_inc(c_kvsave, 16)
                    act.dma_start(kv_d[:, KSIZE:KVSIZE], v_other.rearrange("p s n -> p (s n)")).then_inc(c_kvsave, 16)
                if (j, s) in EVAC:
                    evac(EVAC.index((j, s)))
                if j == 0 and s in ROWS:
                    i = ROWS.index(s)
                    arrived(act, 4 + i)
                    if i == 0:
                        act.wait_ge(c_cps, BATCH)
                    else:
                        act.wait_ge(c_rows, i)
                    act.activation(waste, piece[PLACE[4 + i]], ACT.Abs, accum_out=scd[:, i:i + 1]).then_inc(c_rows, 1)
                if (j, s) == (0, 8):
                    for a in range(2):
                        act.wait_ge(c_lowt, a + 1)
                        act.activation(lowA[:, a * 1024:(a + 1) * 1024], ps[:, a, :].bitcast(BF16), ACT.Copy)\
                            .then_inc(c_lowact, 1)
                if (j, s) == (0, 11):
                    weight_hi(2, 3, wx32_flat, wx)
                if j == 0:
                    for n, slot in enumerate(SUMS):
                        if slot == s:
                            arrived(act, 8 + n)
                            src = piece[PLACE[8 + n]]
                            act.activation(src, src, ACT.Abs, accum_out=wsum[:, n:n + 1]).then_inc(c_asum, 1)

            def t1_hi(g, t):
                need(act, pv_ps, 2, g - 1, 1)
                need(act, t1_ps, TILES, g, t)
                act.activation(xT1[:, 0, :, t * P:(t + 1) * P],
                               att_bank(t).rearrange("p (k n) -> p k n", k=KC), ACT.Copy).then_inc(x1hi, 1)

            def rot_hi(g, hg):
                if hg == 0:
                    need(act, wo_ps, TILES, g - 1, 1)
                need(act, rot_sum, 2, g, hg)
                act.activation(qT[:, 0, hg, :, :].rearrange("p t n -> p (t n)"), ropeu[:, hg, :], ACT.Copy).then_inc(q_hi, 1)

            def exps(g, n):
                if first(g) and n == 0:
                    act.wait_ge(c_kap, 1)
                need(act, s_sub, 4, g, n)
                act.activation(e[:, n, :], e[:, n, :], ACT.Exp, scale=sig[:, :]).then_inc(s_exp, 1)

            def pt_hi(g, n):
                t, hg = S_UNITS[n]
                need(act, pt_ps, 4, g, n)
                act.activation(pt[:, 0, 4 * hg:4 * hg + 4, t * P:(t + 1) * P],
                               att_bank(8 + n).rearrange("p (h n) -> p h n", h=4), ACT.Copy).then_inc(p_hi, 1)

            def pv_hi(g, v):
                need(act, pv_ps, 2, g, v)
                act.activation(ao[:, 0, 2 * v:2 * v + 2, :], att_bank(12 + v).rearrange("p (a n) -> p a n", a=2), ACT.Copy)\
                    .then_inc(ao_hi, 1)

            def t2_hi(g, t):
                need(act, up_ps, FC // 2, g - 1, FC // 2 - 1)
                need(act, t2_ps, TILES, g, t)
                act.activation(xT2[:, 0, :, t * P:(t + 1) * P],
                               att_bank(16 + t).rearrange("p (k n) -> p k n", k=KC), ACT.Copy).then_inc(x2hi, 1)

            def low_first(g):
                need(act, low_ps, 1, g, 0)
                act.activation(tlow[:, :], att_bank(18)[:, 0:G], ACT.Copy).then_inc(low_b, 1)

            def up_act(g, m):
                if first(g) and m == 0:
                    act.wait_ge(c_rsf, 1)
                    act.wait_ge(c_asum, 8)
                need(act, up_ps, FC // 2, g, m)
                for a in range(2):
                    act.activation(rl[:, m % 2, a * G:(a + 1) * G], ps[:, FFN0 + m % 2, a * G:(a + 1) * G], ACT.Relu,
                                   scale=rsf[:, 2 * m + a:2 * m + a + 1]).then_inc(relu, 1)
                if m == 0:
                    need(act, down_ps, TILES, g - 1, 1)
                need(act, relu, FC, g, 2 * m + 1)
                act.activation(hid[:, 0, 2 * m:2 * m + 2, :].rearrange("p c n -> p (c n)"), rl[:, m % 2, :], ACT.Square)\
                    .then_inc(hid_hi, 1)
                if m >= 2:
                    need(act, hid_lo, FC // 2, g, m - 2)
                else:
                    need(act, hid_lo, FC // 2, g - 1, FC // 2 + m - 2)
                act.activation(sq[:, m % 2, :], rl[:, m % 2, :], ACT.Square).then_inc(sq_done, 1)

            def t3_hi(g, t):
                need(act, wx_ps, TILES, g - 1, 1)
                need(act, t3_ps, TILES, g, t)
                act.activation(xT3[:, 0, :, t * P:(t + 1) * P],
                               back_bank(t).rearrange("p (k n) -> p k n", k=KC), ACT.Copy).then_inc(x3hi, 1)

            def t4_out(g, t):
                need(act, w1_ps, 4 * TILES, g - 1, 4 * TILES - 1)
                need(act, t4_ps, TILES, g, t)
                act.activation(q4T[:, :, t * P:(t + 1) * P],
                               back_bank(4 + t).bitcast(F16)[:, 0:D].rearrange("p (k n) -> p k n", k=KC), ACT.Copy)\
                    .then_inc(q4T_done, 1)

            def gelus(g, t):
                need(act, h_done, 4 * TILES, g, 4 * t + 3)
                act.activation(h[:, t, :], h[:, t, :], ACT.Gelu).then_inc(gelu, 1)
                if not (first(g) and t == 0):
                    act.wait_ge(t5_ps, g * (2 * TILES) + 2 * t)
                need(act, gelu, TILES, g, t)
                act.activation(q5[:, :].bitcast(BF16), h[:, t, :], ACT.Square, accum_out=ssq[:, t:t + 1]).then_inc(sqsum, 1)

            def t5_out(g, t):
                if not (first(g) and t == 0):
                    act.wait_ge(w2_ps, g * TILES + t)
                for a in range(2):
                    need(act, t5_ps, 2 * TILES, g, 2 * t + a)
                    act.activation(hT[:, 8 * a:8 * a + 8, :].rearrange("p c n -> p (c n)"),
                                   back_bank((14, 17)[t] + a).bitcast(F16), ACT.Copy).then_inc(hT_done, 1)

            def body(ga, gf, gb, gn):
                for s in range(SLOTS):
                    if gf is not None and s < FC // 2:
                        up_act(gf, s)
                    if ga is not None:
                        if s == SL_T1:
                            for t in range(TILES):
                                t1_hi(ga, t)
                        if s - 1 in SL_Q:
                            rot_hi(ga, SL_Q.index(s - 1))
                        if s in SL_S:
                            for n in (2 * SL_S.index(s), 2 * SL_S.index(s) + 1):
                                exps(ga, n)
                        if s in SL_PT:
                            for n in (2 * SL_PT.index(s), 2 * SL_PT.index(s) + 1):
                                pt_hi(ga, n)
                        if s == SL_PV:
                            for v in range(2):
                                pv_hi(ga, v)
                        if s == SL_T2:
                            for t in range(TILES):
                                t2_hi(ga, t)
                        if s == SL_LOW:
                            low_first(ga)
                    if gb is not None:
                        if s in SL_T3:
                            t3_hi(gb, SL_T3.index(s))
                        if s in SL_T4:
                            t4_out(gb, SL_T4.index(s))
                        if s in (SL_W1[0] + 2, SL_W1[1] + 2):
                            gelus(gb, (SL_W1[0] + 2, SL_W1[1] + 2).index(s))
                        if s in SL_T5:
                            t5_out(gb, SL_T5.index(s))
                    if isinstance(ga, int) and ga < 2:
                        prepare(ga, s)

            prepare_first()
            main_loop(act, body)

        @block.vector
        def _(dve):
            def abs_max(dst, src, done):
                return dve.tensor_reduce(dst, src, axis=AX.X, op=ALU.max, apply_absolute_value=True).then_inc(done, 1)

            def rotate_k(hg):
                dve.wait_ge(c_kps, hg + 1)
                kp = ps[:, 5 + hg, :].rearrange("p (t n) -> p t n", t=2)
                dve.tensor_tensor(krot[:, hg, :].rearrange("p (t n) -> p t n", t=2), kp,
                                  rope[:, 0, :].unsqueeze(1).broadcast_to([P, 2, G]), ALU.mult).then_inc(c_kru, 1)
                dve.tensor_tensor(ktmp[:, hg, 0:G], kp[:, 1, :], rope[:, 1, :], ALU.mult).then_inc(c_kru, 1)
                dve.tensor_tensor(ktmp[:, hg, G:2 * G], kp[:, 0, :], rope[:, 2, :], ALU.mult).then_inc(c_kru, 1)

            def weight_max(col, loaded, count, src):
                dve.wait_ge(loaded, count)
                abs_max(wmax[:, col:col + 1], src, c_wmax)

            def weight_scale(n, a, b):
                dve.wait_ge(c_wmaxa, n + 1)
                dve.tensor_scalar(wmaxa[:, a:b], wmaxa[:, a:b], TINY, 1.0 / TOP, ALU.max, ALU.mult).then_inc(c_wchain, 1)

            def weight_inv(a, b, chain):
                dve.wait_ge(c_wchain, chain)
                dve.reciprocal(winv[:, a:b], wmaxa[:, a:b]).then_inc(c_wscale, 1)

            def weight_lo(n, col, src, dst):
                dve.wait_ge(c_wscale, n + 1)
                dve.wait_ge(c_whi, n + 1)
                flat = dst[:, :, :, :].rearrange("p s k n -> p s (k n)")
                dve.scalar_tensor_tensor(flat[:, 1, :], src, winv[:, col:col + 1], flat[:, 0, :], ALU.mult, ALU.subtract)\
                    .then_inc(c_wlo, 1)

            def k_blocks(b, dst):
                for s in range(2):
                    kin = k16[:, s, :].rearrange("p (a b n) -> p a b n", a=4, b=BATCH)[:, :, b, :]
                    kout = dst[s].rearrange("p (a j n) -> p a j n", a=4, j=4)
                    for j in range(4):
                        last = dve.tensor_scalar(kout[:, :, j, :], kin, mask[:, j:j + 1], None, ALU.mult)
                last.then_inc(c_kblk, 1)

            def v_lo(b, dst):
                dve.wait_ge(c_vhi, b + 1)
                dve.scalar_tensor_tensor(dst[:, 1, :], ps[:, b, :], kvinv[:, 1:2], dst[:, 0, :], ALU.mult, ALU.subtract)\
                    .then_inc(c_vlo, 1)

            def prepare_first():
                dve.wait_ge(c_const, 4)
                dve.tensor_copy(ident16[:, :], ident[:, :]).then_inc(c_id16, 1)
                dve.tensor_copy(identb[:, :], ident[:, :]).then_inc(c_id16, 1)
                dve.wait_ge(d_ctx, 16)
                for b in range(BATCH):
                    dve.tensor_reduce(csum[:, :, b], ctxT[:, :, b * S:(b + 1) * S], axis=AX.X, op=ALU.add).then_inc(c_cs, 1)
                ln1_stats(0)
                dve.wait_ge(d_kr, 16)
                rotate_k(0)
                weight_max(0, d_wq, 16, wq32)
                rotate_k(1)
                ln1_apply(0)
                weight_scale(0, 0, 1)
                weight_inv(0, 1, 1)
                dve.wait_ge(c_krot, 2)
                abs_max(kvmax[:, 0:1], krot.rearrange("p h n -> p (h n)"), c_kvmax)
                weight_lo(0, 0, wq32, wq)
                dve.wait_ge(c_vps, BATCH)
                abs_max(kvmax[:, 1:2], ps[:, 0:2, :].rearrange("p b n -> p (b n)"), c_kvmax)
                dve.wait_ge(c_kvmaxa, 1)
                dve.tensor_scalar(kvmaxa[:, :], kvmaxa[:, :], TINY, 1.0 / TOP, ALU.max, ALU.mult).then_inc(c_kvinv, 1)
                dve.wait_ge(c_kvinv, 1)
                dve.reciprocal(kvinv[:, :], kvmaxa[:, :]).then_inc(c_kvinv, 1)
                dve.wait_ge(c_kvinv, 2)
                dve.tensor_scalar(sig[:, :], wmaxa[:, 0:1], kvmaxa[:, 0:1], HD ** -0.5, ALU.mult, ALU.mult).then_inc(c_kap, 1)
                dve.wait_ge(c_khi, 1)
                dve.scalar_tensor_tensor(k16[:, 1, :], krot.rearrange("p h n -> p (h n)"), kvinv[:, 0:1], k16[:, 0, :],
                                         ALU.mult, ALU.subtract).then_inc(c_klo, 1)
                dve.wait_ge(d_small, 128)
                dve.wait_ge(c_klo, 1)
                k_blocks(0, [kv[:, s * KSIZE // 2:(s + 1) * KSIZE // 2] for s in range(2)])
                v_lo(0, v_now)
                v_lo(1, v_other)

            def thresholds(q):
                kind, i = QUANT[q]
                if kind == "fc":
                    arrived(dve, LOAD_OF[q])
                    src = piece[PLACE[LOAD_OF[q]]].rearrange("p (c n) -> p c n", c=KC)
                    sc, cols = scf[:, 4 * i:4 * i + 4], slice(4 * i, 4 * i + 4)
                    dve.tensor_reduce(sc, src, axis=AX.X, op=ALU.add, apply_absolute_value=True).then_inc(c_scf, 1)
                    dve.wait_ge(c_scf, i + 1)
                else:
                    sc, cols = scd[:, i:i + 1], slice(FC + i, FC + i + 1)
                    dve.wait_ge(c_rows, i + 1)
                dve.tensor_scalar(sc, sc, 1.0 / (D if kind == "fc" else HID), 1e-5, ALU.mult, ALU.max).then_inc(c_scale, 1)
                dve.wait_ge(c_scale, q + 1)
                dve.tensor_scalar(thr[:, cols], sc, 0.5, None, ALU.mult)
                dve.tensor_scalar(nthr[:, cols], sc, -0.5, None, ALU.mult).then_inc(c_thr, 1)

            def signs(q):
                dve.wait_ge(c_pos, q + 1)
                dve.wait_ge(c_thr, q + 1)
                if q >= 2:
                    dve.wait_ge(c_tern, 2 * (q - 1))
                src = piece[PLACE[LOAD_OF[q]]]
                for a, b, _, nt in sign_parts(q):
                    last = dve.scalar_tensor_tensor(neg[q % 2][:, a:b], src[:, a:b], nt, pos[q % 2][:, a:b], ALU.is_lt,
                                                    ALU.subtract)
                last.then_inc(c_quant, 1)

            def v_parts():
                vr = lambda s: vrep[:, s, :, :].rearrange("p k (a r) -> p k a r", r=RANK)
                for s in range(2):
                    for k in range(KC):
                        vin = vT_sb[:, k, :].unsqueeze(1).broadcast_to([P, REP, RANK])
                        if s == 0:
                            last = dve.tensor_scalar(vr(0)[:, k], vin, winv[:, 2:3], None, ALU.mult)
                        else:
                            last = dve.scalar_tensor_tensor(vr(1)[:, k], vin, winv[:, 2:3], vr(0)[:, k], ALU.mult,
                                                            ALU.subtract)
                    last.then_inc(c_vrep, 1)
                    dve.wait_ge(c_vrep, s + 1)

            def low_rank():
                dve.wait_ge(c_scale, 4)
                dve.reciprocal(gsf[:, :], scf[:, :]).then_inc(c_low, 1)
                dve.wait_ge(c_low, 1)
                dve.tensor_scalar(gsf[:, :], gsf[:, :], gate[:, :], wmaxa[:, 2:3], ALU.mult, ALU.mult).then_inc(c_low, 1)
                dve.wait_ge(c_low, 2)
                dve.wait_ge(c_lowps, 1)
                dve.tensor_tensor(low, lowprod, gsf[:, :].unsqueeze(2).broadcast_to([P, FC, RANK]), ALU.mult).then_inc(c_low, 1)
                dve.wait_ge(c_low, 3)
                dve.wait_ge(c_lowzero, 1)
                dve.tensor_copy(lowF[:, :, 0, :], low).then_inc(c_low, 1)
                dve.wait_ge(c_low, 4)
                dve.tensor_tensor(lowres, low, lowF[:, :, 0, :], ALU.subtract).then_inc(c_low, 1)
                dve.wait_ge(c_low, 5)
                dve.tensor_copy(lowF[:, :, 1, :], lowres).then_inc(c_low, 1)
                dve.wait_ge(c_low, 6)
                dve.tensor_tensor(lowF[:, :, 4, :], lowres, lowF[:, :, 1, :], ALU.subtract)
                dve.tensor_copy(lowF[:, :, 2, :], lowF[:, :, 0, :])
                dve.tensor_copy(lowF[:, :, 6, :], lowF[:, :, 0, :])
                dve.tensor_copy(lowF[:, :, 3, :], lowF[:, :, 1, :]).then_inc(c_lowF, 1)
                dve.tensor_reduce(bnd[:, :], low, axis=AX.X, op=ALU.add, apply_absolute_value=True).then_inc(c_bnd, 1)
                dve.wait_ge(c_bnd, 1)
                dve.tensor_scalar(bnd[:, :], bnd[:, :], D * TOP, float(D), ALU.mult, ALU.add).then_inc(c_bnd, 1)
                dve.wait_ge(c_bnd, 2)
                dve.tensor_tensor(bnd[:, :], bnd[:, :], scf[:, :], ALU.mult).then_inc(c_bnd, 1)
                dve.wait_ge(c_bnd, 3)
                dve.tensor_reduce(bmax[:, :], bnd[:, :], axis=AX.X, op=ALU.max).then_inc(c_bnd, 1)

            def hidden_scale():
                dve.wait_ge(c_bndmax, 1)
                dve.tensor_scalar(irho[:, :], bmaxa[:, :], 1.0 / RMAX, None, ALU.mult).then_inc(c_rho, 1)
                dve.wait_ge(c_rho, 1)
                dve.reciprocal(rho[:, :], irho[:, :]).then_inc(c_rho, 1)
                dve.wait_ge(c_rho, 2)
                dve.tensor_scalar(rsf[:, :], scf[:, :], rho[:, :], None, ALU.mult).then_inc(c_rsf, 1)

            def mix_row():
                for b in range(BATCH):
                    dve.wait_ge(c_cps, b + 1)
                    dve.scalar_tensor_tensor(cb[:, b, :], ps[:, b, :], 1.0 / S, cb_now[:, :], ALU.mult, ALU.add).then_inc(c_cs, 1)
                for b in range(BATCH):
                    dve.wait_ge(c_cs, 3 + b)
                    dve.tensor_scalar(cb[:, b, :], cb[:, b, :], tg[:, 1:2], None, ALU.mult).then_inc(c_cb, 1)

            def prepare(j, s):
                if (j, s) in SIGN:
                    signs(SIGN.index((j, s)))
                if (j, s) in THR:
                    thresholds(THR.index((j, s)))
                if (j, s) == (0, 0):
                    weight_max(1, d_wo, 16, wo32)
                    weight_max(2, d_small, 128, vT_sb.rearrange("p k r -> p (k r)"))
                if (j, s) == (0, 1):
                    weight_scale(1, 1, 3)
                    weight_inv(1, 3, 2)
                    dve.wait_ge(c_tanh, 1)
                    dve.tensor_scalar(kapo[:, :], wmaxa[:, 1:2], kvmaxa[:, 1:2], tg[:, 0:1], ALU.mult, ALU.mult).then_inc(c_kap, 1)
                    k_blocks(1, k_other)
                if (j, s) == (0, 3):
                    weight_lo(1, 1, wo32, wo)
                if (j, s) == (0, 5):
                    mix_row()
                if (j, s) == (0, 6):
                    low_rank()
                if (j, s) == (0, 7):
                    v_parts()
                if (j, s) == (0, 8):
                    weight_max(3, d_wx, 16, wx32_flat)
                if (j, s) == (0, 9):
                    hidden_scale()
                if (j, s) == (0, 10):
                    weight_scale(2, 3, 4)
                    weight_inv(3, 4, 3)
                    dve.tensor_scalar(kapx[:, :], wmaxa[:, 3:4], tg[:, 1:2], None, ALU.mult).then_inc(c_kap, 1)
                if (j, s) == (0, 12):
                    weight_lo(2, 3, wx32_flat, wx)
                    dve.wait_ge(c_scale, 8)
                    for k in range(KC):
                        last = dve.tensor_scalar(diag[:, k * P:(k + 1) * P], ident[:, :], scd[:, k:k + 1], None, ALU.mult)
                    last.then_inc(c_scd, 1)
                    dve.tensor_scalar(c1[:, :], irho[:, :], irho[:, :], tg[:, 2:3], ALU.mult, ALU.mult).then_inc(c_scd, 1)
                if (j, s) == (0, 14):
                    dve.wait_ge(c_scd, 2)
                    dve.wait_ge(c_scps, 1)
                    dve.tensor_scalar(scbc[:, :], ps[:, 0, :], c1[:, :], None, ALU.mult).then_inc(c_sc, 1)
                    dve.tensor_scalar(b2bc[:, :], b2bc[:, :], tg[:, 3:4], None, ALU.mult).then_inc(c_b2, 1)
                if (j, s) == (0, 15):
                    dve.wait_ge(c_asumps, 1)
                    dve.tensor_reduce(wmean[:, :], ps[:, 7, 0:8].rearrange("p (w n) -> p w n", w=2), axis=AX.X, op=ALU.add)\
                        .then_inc(c_mean, 1)
                    dve.wait_ge(c_mean, 1)
                    dve.tensor_scalar(wmean[:, :], wmean[:, :], 1.0 / (D * HID), 1e-5, ALU.mult, ALU.max).then_inc(c_mean, 1)
                    dve.wait_ge(c_mean, 2)
                    dve.tensor_scalar(aw2t[:, :], wmean[:, 1:2], tg[:, 3:4], None, ALU.mult).then_inc(c_mean, 1)
                    dve.tensor_scalar(thr1[:, :], wmean[:, :], 0.5, None, ALU.mult)
                    dve.tensor_scalar(nthr1[:, :], wmean[:, :], -0.5, None, ALU.mult).then_inc(c_thr, 8)

            def ln_stats(done, g, n, t, src, scale, add):
                dve.bn_stats(st[:, n, t, :], src).then_inc(done, 1)
                need(dve, done, 3 * TILES, g, 3 * t)
                dve.memset(pad[:, :], 0.0)
                dve.bn_aggr(mv[:, n, t, :], st[:, n, t, :]).then_inc(done, 1)
                need(dve, done, 3 * TILES, g, 3 * t + 1)
                dve.tensor_scalar(ve[:, n, t:t + 1], mv[:, n, t, 1:2], scale, add, ALU.mult, ALU.add).then_inc(done, 1)

            def ln_apply(rsem, done, g, n, t, src, dst):
                need(dve, rsem, TILES, g, t)
                dve.tensor_scalar(dst, src, mv[:, n, t, 0:1], rs[:, n, t:t + 1], ALU.subtract, ALU.mult).then_inc(done, 1)

            def lo(dst, src, hi, done):
                dve.tensor_tensor(dst, src, hi, ALU.subtract).then_inc(done, 1)

            def ln1_stats(g):
                dve.wait_ge(xa_in, g * 16 + 16)
                for t in range(TILES):
                    ln_stats(ln1, g, 0, t, xa[:, t, :], 1.0, EPS)

            def ln1_apply(g):
                for t in range(TILES):
                    ln_apply(rs1, xn1, g, 0, t, xa[:, t, :], xa[:, t, :])

            def t1_lo(g, t):
                need(dve, x1hi, TILES, g, t)
                c = slice(t * P, (t + 1) * P)
                lo(xT1[:, 1, :, c], att_bank(t).rearrange("p (k n) -> p k n", k=KC), xT1[:, 0, :, c], x1lo)

            def rot(g, hg):
                if hg == 0:
                    dve.wait_ge(rope_in, g * 16 + 16)
                    need(dve, t2_ps, TILES, g - 1, 1)
                need(dve, q_ps, 2, g, hg)
                qp = att_bank(2 + hg).rearrange("p (t n) -> p t n", t=2)
                dve.tensor_tensor(ropeu[:, hg, :].rearrange("p (t n) -> p t n", t=2), qp,
                                  rope[:, 0, :].unsqueeze(1).broadcast_to([P, 2, G]), ALU.mult).then_inc(rot_mul, 1)
                dve.tensor_tensor(ropew[:, hg, 0:G], qp[:, 1, :], rope[:, 1, :], ALU.mult).then_inc(rot_mul, 1)
                dve.tensor_tensor(ropew[:, hg, G:2 * G], qp[:, 0, :], rope[:, 2, :], ALU.mult).then_inc(rot_mul, 1)

            def rot_lo(g, hg):
                need(dve, q_hi, 2, g, hg)
                flat = qT[:, :, hg, :, :].rearrange("p s t n -> p s (t n)")
                lo(flat[:, 1, :], ropeu[:, hg, :], flat[:, 0, :], q_lo)

            def s_view(n):
                return e[:, n, :].rearrange("p (h s) -> p h s", h=4)

            def soft_max(g, n):
                need(dve, s_ps, 4, g, n)
                scores = att_bank(4 + n).rearrange("p (h s) -> p h s", h=4)
                dve.tensor_reduce(nmx[:, n, :], scores, axis=AX.X, op=ALU.max, negate=True).then_inc(s_max, 1)
                need(dve, s_max, 4, g, n)
                dve.tensor_tensor(s_view(n), scores, nmx[:, n, :].unsqueeze(2).broadcast_to([P, 4, S]), ALU.add)\
                    .then_inc(s_sub, 1)

            def soft_sum(g, n):
                need(dve, s_exp, 4, g, n)
                dve.tensor_reduce(esum[:, n, :], s_view(n), axis=AX.X, op=ALU.add).then_inc(s_sum, 1)
                need(dve, s_sum, 4, g, n)
                dve.reciprocal(einv[:, n, :], esum[:, n, :]).then_inc(s_inv, 1)

            def pt_lo(g, n):
                t, hg = S_UNITS[n]
                need(dve, p_hi, 4, g, n)
                part = pt[:, :, 4 * hg:4 * hg + 4, t * P:(t + 1) * P]
                lo(part[:, 1], att_bank(8 + n).rearrange("p (h n) -> p h n", h=4), part[:, 0], p_lo)

            def pv_lo(g, v):
                need(dve, ao_hi, 2, g, v)
                part = ao[:, :, 2 * v:2 * v + 2, :]
                lo(part[:, 1], att_bank(12 + v).rearrange("p (a n) -> p a n", a=2), part[:, 0], ao_lo)

            def x1_out(g, t):
                if t == 0:
                    dve.wait_ge(xb_in, g * 16 + 16)
                    if not first(g):
                        dve.wait_ge(r1_copied, g * 16)
                    if first(g):
                        dve.wait_ge(c_kap, 2)
                need(dve, wo_ps, TILES, g, t)
                dve.scalar_tensor_tensor(r1[:, t, :], att_bank(14 + t), kapo[:, :], xb[:, t, :], ALU.mult, ALU.add)\
                    .then_inc(x1_done, 1)
                need(dve, x1_done, TILES, g, t)
                ln_stats(ln2, g, 1, t, r1[:, t, :], 1.0, EPS)

            def ln2_apply(g):
                for t in range(TILES):
                    ln_apply(rs2, xn2_done, g, 1, t, r1[:, t, :], xn2[:, t, :])

            def t2_lo(g, t):
                need(dve, x2hi, TILES, g, t)
                c = slice(t * P, (t + 1) * P)
                lo(xT2[:, 1, :, c], att_bank(16 + t).rearrange("p (k n) -> p k n", k=KC), xT2[:, 0, :, c], x2lo)

            def low_parts(g):
                need(dve, low_b, 1, g, 0)
                dve.tensor_tensor(tres[:, :], att_bank(18)[:, 0:G], tlow[:, :], ALU.subtract).then_inc(low_r, 1)
                need(dve, low_r, 2, g, 0)
                dve.tensor_copy(tlow[32:64, :], tres[32:64, :])
                dve.tensor_copy(tb2[96:128, :], tres[96:128, :]).then_inc(low_r, 1)
                need(dve, low_r, 2, g, 1)
                dve.tensor_tensor(tlow[96:128, :], tres[96:128, :], tb2[96:128, :], ALU.subtract).then_inc(low_done, 1)

            def hid_low(g, m):
                need(dve, sq_done, FC // 2, g, m)
                flat = hid[:, :, 2 * m:2 * m + 2, :].rearrange("p s c n -> p s (c n)")
                lo(flat[:, 1, :], sq[:, m % 2, :], flat[:, 0, :], hid_lo)

            def x2_out(g, t):
                if first(g) and t == 0:
                    dve.wait_ge(c_sc, 1)
                need(dve, down_ps, TILES, g, t)
                dve.tensor_tensor(r2[:, t, :], ps[:, FFN0 + t, :], scbc[:, :], ALU.mult).then_inc(down_mul, 1)
                if t == 0:
                    dve.wait_ge(r1_copied, g * 16 + 16)
                need(dve, down_mul, TILES, g, t)
                dve.tensor_tensor(r2[:, t, :], r2[:, t, :], r1b[:, t, :], ALU.add).then_inc(x2_done, 1)
                need(dve, x2_done, TILES, g, t)
                ln_stats(ln3, g, 2, t, r2[:, t, :], 1.0, EPS)

            def ln3_apply(g, t):
                ln_apply(rs3, xn3, g, 2, t, r2[:, t, :], x3n[:, t, :])

            def t3_lo(g, t):
                need(dve, x3hi, TILES, g, t)
                c = slice(t * P, (t + 1) * P)
                lo(xT3[:, 1, :, c], back_bank(t).rearrange("p (k n) -> p k n", k=KC), xT3[:, 0, :, c], x3lo)

            def x3_out(g, t):
                if not first(g):
                    dve.wait_ge(out_stored[t], g * 16)
                if first(g) and t == 0:
                    dve.wait_ge(c_kap, 3)
                need(dve, x2c, TILES, g, t)
                need(dve, wx_ps, TILES, g, t)
                dve.scalar_tensor_tensor(r3[:, t, :], back_bank(2 + t), kapx[:, :], r2[:, t, :], ALU.mult, ALU.add)\
                    .then_inc(x3_done, 1)
                need(dve, x3_done, TILES, g, t)
                ln_stats(ln4, g, 3, t, r3[:, t, :], 1.0 + EPS, EPS * EPS)
                dve.tensor_scalar(x3n[:, t, :], r3[:, t, :], mv[:, 3, t, 0:1], None, ALU.subtract).then_inc(z4, 1)
                need(dve, z4, 6 * TILES, g, 6 * t)
                abs_max(amax[:, 0, t:t + 1], x3n[:, t, :], z4)

            def quant_scales(sem_z, base, per, a, g, t, rsem, n, mean):
                need(dve, rsem, TILES, g, t)
                need(dve, sem_z, per, g, base - 1)
                dve.tensor_scalar(zmax[:, a, t:t + 1], amax[:, a, t:t + 1], rs[:, n, t:t + 1], 1e-5, ALU.mult, ALU.max)\
                    .then_inc(sem_z, 1)
                need(dve, sem_z, per, g, base)
                dve.reciprocal(zinv[:, a, t:t + 1], zmax[:, a, t:t + 1]).then_inc(sem_z, 1)
                need(dve, sem_z, per, g, base + 1)
                dve.tensor_scalar(qsc[:, a, t:t + 1], zinv[:, a, t:t + 1], rs[:, n, t:t + 1], 127.0, ALU.mult, ALU.mult)\
                    .then_inc(sem_z, 1)
                dve.tensor_scalar(dqs[:, a, t:t + 1], zmax[:, a, t:t + 1], mean, 1.0 / 127.0, ALU.mult, ALU.mult)\
                    .then_inc(sem_z, 1)
                need(dve, sem_z, per, g, base + 3)

            def q4_out(g, t):
                if first(g) and t == 0:
                    dve.wait_ge(c_mean, 3)
                quant_scales(z4, 6 * t + 2, 6 * TILES, 0, g, t, rs4, 3, wmean[:, 0:1])
                dve.tensor_scalar(x3n[:, t, :], x3n[:, t, :], qsc[:, 0, t:t + 1], MAGIC, ALU.mult, ALU.add).then_inc(q4_done, 1)
                need(dve, q4_done, 2 * TILES, g, 2 * t)
                dve.tensor_scalar(q4[:, t, :], x3n[:, t, :], MAGIC, None, ALU.subtract).then_inc(q4_done, 1)

            def h_out(g, t, n):
                need(dve, w1_ps, 4 * TILES, g, 4 * t + n)
                if first(g) and t == 0 and n == 0:
                    dve.wait_ge(d_b1, 16)
                c = slice(n * 512, (n + 1) * 512)
                dve.scalar_tensor_tensor(h[:, t, c], back_bank(6 + 4 * t + n), dqs[:, 0, t:t + 1], b1bc[:, c],
                                         ALU.mult, ALU.add).then_inc(h_done, 1)

            def q5_scales(g, t):
                need(dve, gelu, TILES, g, t)
                abs_max(amax[:, 1, t:t + 1], h[:, t, :], z5)
                need(dve, sqsum, TILES, g, t)
                dve.tensor_scalar(ve[:, 4, t:t + 1], ssq[:, t:t + 1], 1.0 / HID, EPS, ALU.mult, ALU.add).then_inc(z5, 1)

            def q5_out(g, t):
                quant_scales(z5, 6 * t + 2, 6 * TILES, 1, g, t, rs5, 4, aw2t[:, :])
                dve.tensor_scalar(h[:, t, :], h[:, t, :], qsc[:, 1, t:t + 1], MAGIC, ALU.mult, ALU.add).then_inc(q5_done, 1)
                need(dve, q5_done, 2 * TILES, g, 2 * t)
                dve.tensor_scalar(q5[:, :], h[:, t, :], MAGIC, None, ALU.subtract).then_inc(q5_done, 1)

            def x4_out(g, t):
                need(dve, x3b, TILES, g, t)
                need(dve, w2_ps, TILES, g, t)
                dve.scalar_tensor_tensor(r3[:, t, :], back_bank((16, 19)[t]), dqs[:, 1, t:t + 1], r3[:, t, :],
                                         ALU.mult, ALU.add).then_inc(out_done, 1)

            def body(ga, gf, gb, gn):
                for s in range(SLOTS):
                    if gf is not None and 1 <= s <= FC // 2:
                        hid_low(gf, s - 1)
                    if ga is not None:
                        if s == SL_T1:
                            for t in range(TILES):
                                t1_lo(ga, t)
                        if s - 1 in SL_Q:
                            rot_lo(ga, SL_Q.index(s - 1))
                        if s in SL_Q:
                            rot(ga, SL_Q.index(s))
                        if s - 1 in SL_S:
                            for n in (2 * SL_S.index(s - 1), 2 * SL_S.index(s - 1) + 1):
                                soft_sum(ga, n)
                        if s in SL_S:
                            for n in (2 * SL_S.index(s), 2 * SL_S.index(s) + 1):
                                soft_max(ga, n)
                        if s in SL_PT:
                            for n in (2 * SL_PT.index(s), 2 * SL_PT.index(s) + 1):
                                pt_lo(ga, n)
                        if s == SL_PV:
                            for v in range(2):
                                pv_lo(ga, v)
                        if s == SL_WO:
                            for t in range(TILES):
                                x1_out(ga, t)
                        if s == SL_WO + 1:
                            ln2_apply(ga)
                        if s == SL_T2:
                            for t in range(TILES):
                                t2_lo(ga, t)
                        if s == SL_LOW:
                            low_parts(ga)
                    if gb is not None:
                        if s in SL_T3:
                            t3_lo(gb, SL_T3.index(s))
                        if s - 1 in SL_WX:
                            q4_out(gb, SL_WX.index(s - 1))
                        if s in SL_WX:
                            x3_out(gb, SL_WX.index(s))
                        for t in range(TILES):
                            if s in (SL_W1[t], SL_W1[t] + 1):
                                n0 = 2 * (s - SL_W1[t])
                                h_out(gb, t, n0)
                                h_out(gb, t, n0 + 1)
                            if s == SL_W1[t] + 2:
                                q5_scales(gb, t)
                            if s == SL_W1[t] + 3:
                                q5_out(gb, t)
                            if s == SL_W2[t]:
                                x4_out(gb, t)
                    if gf is not None and s - 1 in SL_X2:
                        ln3_apply(gf, SL_X2.index(s - 1))
                    if gf is not None and s in SL_X2:
                        x2_out(gf, SL_X2.index(s))
                    if gn is not None and s == SL_LN1:
                        ln1_stats(gn)
                    if gn is not None and s == SL_LN1 + 1:
                        ln1_apply(gn)
                    if isinstance(ga, int) and ga < 2:
                        prepare(ga, s)
                if gf is not None:
                    ln3_apply(gf, 1)

            prepare_first()
            main_loop(dve, body)

        @block.tensor
        def _(pe):
            def prepare_first():
                pe.wait_ge(d_ctx, 16)
                pe.wait_ge(d_wk, 16)
                for hg in range(2):
                    for t in range(2):
                        c = (2 * hg + t) * P
                        for k in range(KC):
                            mm = pe.matmul(ps[:, 5 + hg, t * G:(t + 1) * G], wkv32[:, k, c:c + P], ctxT[:, k, :],
                                           start=(k == 0), stop=(k == KC - 1))
                    mm.then_inc(c_kps, 1)
                pe.wait_ge(d_wv, 16)
                for b in range(BATCH):
                    for k in range(KC):
                        mm = pe.matmul(ps[:, b, :], ctxT[:, k, b * S:(b + 1) * S], wkv32[:, k, D:2 * D],
                                       start=(k == 0), stop=(k == KC - 1))
                    mm.then_inc(c_vps, 1)
                pe.wait_ge(c_id16, 2)

            def ternary(q):
                kind, i = QUANT[q]
                pe.wait_ge(c_quant, q + 1)
                for a in range(2):
                    if q >= 1:
                        pe.wait_ge(c_quantp, 2 * q + a - 1)
                    for n in range(8 * a, 8 * a + 8):
                        src = (n % KC) * D + (n // KC) * P if kind in ("fc", "w1") else n * P
                        mm = pe.transpose(ps[:, 5 + a, :].bitcast(F16)[:, n % 8 * P:(n % 8 + 1) * P],
                                          neg[q % 2][:, src:src + P], ident16[:, :])
                    mm.then_inc(c_tern, 1)

            def prepare(j, s):
                if (j, s) == (0, 1):
                    pe.wait_ge(d_u, 16)
                    pe.wait_ge(d_small, 128)
                    for c in range(FC):
                        mm = pe.matmul(lowprod[:, c, :], uT[:, c * P:(c + 1) * P], fb_sb, start=True, stop=True)
                    mm.then_inc(c_lowps, 1)
                if (j, s) == (0, 2):
                    pe.wait_ge(d_wc, 16)
                    pe.wait_ge(c_csb, 1)
                    pe.wait_ge(c_vlo, BATCH)
                    for b in range(BATCH):
                        for k in range(KC):
                            mm = pe.matmul(ps[:, b, :], csb[:, b, k, :], wc32[:, k, :], start=(k == 0), stop=(k == KC - 1))
                        mm.then_inc(c_cps, 1)
                if (j, s) in TERN:
                    ternary(TERN.index((j, s)))
                if (j, s) == (0, 7):
                    pe.wait_ge(c_cb, BATCH)
                    pe.wait_ge(c_lowF, 1)
                    for c in range(FC):
                        mm = pe.transpose(ps[:, c // 8, :].bitcast(BF16)[:, c % 8 * P:(c % 8 + 1) * P],
                                          lowF[:, c, :, :].rearrange("p a r -> p (a r)"), identb[:, :])
                        if c % 8 == 7:
                            mm.then_inc(c_lowt, 1)
                if (j, s) == (0, 13):
                    pe.wait_ge(c_lowact, 1)
                    pe.wait_ge(c_scd, 1)
                    pe.matmul(ps[:, 0, :], ones[:, :], diag, start=True, stop=True).then_inc(c_scps, 1)
                if (j, s) == (0, 15):
                    pe.wait_ge(c_asum, 8)
                    pe.wait_ge(c_low, 3)
                    pe.matmul(ps[:, 7, 0:8], ones[:, :], wsum[:, :], start=True, stop=True).then_inc(c_asumps, 1)

            def t1(g, t):
                if t == 0:
                    need(pe, low_r, 2, g - 1, 0)
                else:
                    need(pe, x2lo, TILES, g - 1, 0)
                need(pe, xn1, TILES, g, t)
                for k in range(KC):
                    mm = pe.transpose(att_bank(t)[:, k * P:(k + 1) * P], xa[:, t, k * P:(k + 1) * P], ident[:, :])
                mm.then_inc(t1_ps, 1)

            def q_proj(g, hg):
                if first(g) and hg == 0:
                    pe.wait_ge(c_wlo, 1)
                if hg == 0:
                    need(pe, x2lo, TILES, g - 1, 1)
                    need(pe, x1lo, TILES, g, 1)
                else:
                    need(pe, x1lo, TILES, g, 0)
                for a in range(2):
                    c = (2 * hg + a) * P
                    for n, (ws, xs) in enumerate(PARTS):
                        for k in range(KC):
                            mm = pe.matmul(att_bank(2 + hg)[:, a * G:(a + 1) * G], wq[:, ws, k, c:c + P], xT1[:, xs, k, :],
                                           start=(n == 0 and k == 0), stop=(n == 2 and k == KC - 1))
                mm.then_inc(q_ps, 1)

            def scores(g, n):
                t, hg = S_UNITS[n]
                if first(g) and n == 0:
                    pe.wait_ge(c_kblk, 1)
                if n == 0:
                    need(pe, x1lo, TILES, g, 1)
                elif n < 3:
                    need(pe, rot_mul, 6, g, 3 * n - 1)
                else:
                    need(pe, s_sub, 4, g, n - 3)
                need(pe, q_lo, 2, g, hg)
                for m, (qs, ks) in enumerate(PARTS):
                    for a in range(2):
                        mm = pe.matmul(att_bank(4 + n), qT[:, qs, hg, a, t * P:(t + 1) * P], k_now[:, ks, hg, a, :],
                                       start=(m == 0 and a == 0), stop=(m == 2 and a == 1))
                mm.then_inc(s_ps, 1)

            def p_transpose(g, n):
                if n < 3:
                    need(pe, s_sub, 4, g, n + 1)
                else:
                    need(pe, p_lo, 4, g, n - 3)
                need(pe, s_norm, 4, g, n)
                for j in range(4):
                    mm = pe.transpose(att_bank(8 + n)[:, j * P:(j + 1) * P], e[:, n, j * S:(j + 1) * S], ident[:, :])
                mm.then_inc(pt_ps, 1)

            def p_v(g, v):
                if first(g) and v == 0:
                    pe.wait_ge(c_vlo, 1)
                need(pe, p_lo, 4, g, 3)
                for a in range(2):
                    for n, (vs, xs) in enumerate(PARTS):
                        for o in range(2):
                            head = 4 * v + 2 * a + o
                            mm = pe.matmul(att_bank(12 + v)[o * HD:(o + 1) * HD, a * G:(a + 1) * G],
                                           v_now[:, vs, head * HD:(head + 1) * HD], pt[:, xs, head, :],
                                           start=(n == 0), stop=(n == 2), tile_position=(0, o * HD))
                mm.then_inc(pv_ps, 1)

            def out_proj(g, t):
                if first(g) and t == 0:
                    pe.wait_ge(c_wlo, 2)
                need(pe, ao_lo, 2, g, 1)
                for n, (xs, ws) in enumerate(PARTS):
                    for k in range(KC):
                        mm = pe.matmul(att_bank(14 + t), ao[:, xs, k, t * P:(t + 1) * P], wo[:, ws, k, :],
                                       start=(n == 0 and k == 0), stop=(n == 2 and k == KC - 1))
                mm.then_inc(wo_ps, 1)

            def t2(g, t):
                if t == 1:
                    need(pe, x1_done, TILES, g, 0)
                need(pe, xn2_done, TILES, g, t)
                for k in range(KC):
                    mm = pe.transpose(att_bank(16 + t)[:, k * P:(k + 1) * P], xn2[:, t, k * P:(k + 1) * P], ident[:, :])
                mm.then_inc(t2_ps, 1)

            def low_rows(g):
                if first(g):
                    pe.wait_ge(c_vrep, 2)
                need(pe, x1_done, TILES, g, 1)
                need(pe, x2lo, TILES, g, 1)
                for n, (vs, xs) in enumerate(PARTS):
                    for k in range(KC):
                        mm = pe.matmul(att_bank(18)[:, 0:G], vrep[:, vs, k, :], xT2[:, xs, k, :],
                                       start=(n == 0 and k == 0), stop=(n == 2 and k == KC - 1))
                mm.then_inc(low_ps, 1)

            def up(g, m):
                if first(g) and m == 0:
                    pe.wait_ge(c_quantp, 8)
                    pe.wait_ge(c_lowact, 2)
                    pe.wait_ge(c_sc, 1)
                if m == 0:
                    need(pe, low_done, 1, g, 0)
                if m < 2:
                    need(pe, down_mul, TILES, g - 1, m)
                else:
                    need(pe, relu, FC, g, 2 * m - 3)
                for a in range(2):
                    f = 2 * m + a
                    dst = ps[:, FFN0 + m % 2, a * G:(a + 1) * G]
                    pe.matmul(dst, lowA[:, f * P:(f + 1) * P], tlow[:, :], start=True, stop=False)
                    for xs in range(2):
                        for k in range(KC):
                            mm = pe.matmul(dst, fcT[:, k, f * P:(f + 1) * P], xT2[:, xs, k, :], start=False,
                                           stop=(xs == 1 and k == KC - 1))
                mm.then_inc(up_ps, 1)

            def down(g, t, piece_of_4):
                if first(g) and piece_of_4 == 0:
                    pe.wait_ge(c_quantp, 16)
                if piece_of_4 == 0:
                    need(pe, relu, FC, g, FC - 3 + 2 * t)
                need(pe, hid_lo, FC // 2, g, 2 * piece_of_4 + 1)
                pe.ldweights(hid[:, 0, 4 * piece_of_4, t * P:(t + 1) * P], tile_position=(0, 0))
                for c in range(4 * piece_of_4, 4 * piece_of_4 + 4):
                    for xs in range(2):
                        mm = pe.matmul(ps[:, FFN0 + t, :], hid[:, xs, c, t * P:(t + 1) * P], pjT[:, c, :],
                                       start=(c == 0 and xs == 0), stop=(c == FC - 1 and xs == 1))
                if piece_of_4 == 3:
                    mm.then_inc(down_ps, 1)

            def t3(g, t):
                if first(g) and t == 0:
                    pe.wait_ge(c_quantp, 32)
                if t == 0:
                    need(pe, hT_done, 2 * TILES, g - 1, 3)
                else:
                    need(pe, out_done, TILES, g - 1, 1)
                need(pe, xn3, TILES, g, t)
                for k in range(KC):
                    mm = pe.transpose(back_bank(t)[:, k * P:(k + 1) * P], x3n[:, t, k * P:(k + 1) * P], ident[:, :])
                mm.then_inc(t3_ps, 1)

            def mix(g, t):
                if first(g) and t == 0:
                    pe.wait_ge(c_wlo, 3)
                need(pe, x3lo, TILES, g, t)
                for n, (xs, ws) in enumerate(PARTS):
                    for k in range(KC):
                        mm = pe.matmul(back_bank(2 + t), xT3[:, xs, k, t * P:(t + 1) * P], wx[:, ws, k, :],
                                       start=(n == 0 and k == 0), stop=(n == 2 and k == KC - 1))
                mm.then_inc(wx_ps, 1)

            def t4(g, t):
                if t == 0:
                    need(pe, x3lo, TILES, g, 1)
                else:
                    need(pe, x3_done, TILES, g, 0)
                need(pe, q4_done, 2 * TILES, g, 2 * t + 1)
                for k in range(KC):
                    mm = pe.transpose(back_bank(4 + t).bitcast(F16)[:, k * P:(k + 1) * P], q4[:, t, k * P:(k + 1) * P],
                                      ident16[:, :])
                mm.then_inc(t4_ps, 1)

            def w1_up(g, t, n):
                u = 4 * t + n
                if u == 0:
                    need(pe, x3_done, TILES, g, 1)
                    need(pe, q4T_done, TILES, g, 0)
                elif u == 2:
                    need(pe, q4T_done, TILES, g, 1)
                elif u >= 3:
                    need(pe, h_done, 4 * TILES, g, u - 3)
                    if u == 4:
                        need(pe, q4T_done, TILES, g, 1)
                pe.ldweights(q4T[:, 0, t * P:(t + 1) * P], tile_position=(0, 0))
                for k in range(KC):
                    mm = pe.matmul(back_bank(6 + u), q4T[:, k, t * P:(t + 1) * P], w1T[:, k, n * 512:(n + 1) * 512],
                                   start=(k == 0), stop=(k == KC - 1))
                mm.then_inc(w1_ps, 1)

            def t5(g, t):
                need(pe, q5_done, 2 * TILES, g, 2 * t + 1)
                for a in range(2):
                    if t == 0:
                        need(pe, h_done, 4 * TILES, g, 5 + a)
                    else:
                        need(pe, hT_done, 2 * TILES, g, a)
                    for c in range(8):
                        f = (8 * a + c) * P
                        mm = pe.transpose(back_bank((14, 17)[t] + a).bitcast(F16)[:, c * P:(c + 1) * P], q5[:, f:f + P],
                                          ident16[:, :])
                    mm.then_inc(t5_ps, 1)

            def w2_down(g, t):
                if t == 0:
                    need(pe, h_done, 4 * TILES, g, 7)
                else:
                    need(pe, out_done, TILES, g, 0)
                need(pe, hT_done, 2 * TILES, g, 2 * t + 1)
                pe.ldweights(hT[:, 0, :], tile_position=(0, 0))
                for c in range(FC):
                    mm = pe.matmul(back_bank((16, 19)[t]), hT[:, c, :], w2T[:, c, :], start=(c == 0), stop=(c == FC - 1))
                mm.then_inc(w2_ps, 1)

            def body(ga, gf, gb, gn):
                for s in range(SLOTS):
                    if gf is not None:
                        if s < FC // 2:
                            up(gf, s)
                        else:
                            down(gf, (s - FC // 2) // 4, s % 4)
                    if ga is not None:
                        if s == SL_T1:
                            for t in range(TILES):
                                t1(ga, t)
                        if s in SL_Q:
                            q_proj(ga, SL_Q.index(s))
                        if s in SL_S:
                            for n in (2 * SL_S.index(s), 2 * SL_S.index(s) + 1):
                                scores(ga, n)
                        if s in SL_PT:
                            for n in (2 * SL_PT.index(s), 2 * SL_PT.index(s) + 1):
                                p_transpose(ga, n)
                        if s == SL_PV:
                            for v in range(2):
                                p_v(ga, v)
                        if s == SL_WO:
                            for t in range(TILES):
                                out_proj(ga, t)
                        if s == SL_T2:
                            for t in range(TILES):
                                t2(ga, t)
                        if s == SL_LOW:
                            low_rows(ga)
                    if gb is not None:
                        if s in SL_T3:
                            t3(gb, SL_T3.index(s))
                        if s in SL_WX:
                            mix(gb, SL_WX.index(s))
                        if s in SL_T4:
                            t4(gb, SL_T4.index(s))
                        for t in range(TILES):
                            if s in (SL_W1[t], SL_W1[t] + 1):
                                n0 = 2 * (s - SL_W1[t])
                                w1_up(gb, t, n0)
                                w1_up(gb, t, n0 + 1)
                        if s in SL_W2:
                            w2_down(gb, SL_W2.index(s))
                        if s in SL_T5:
                            t5(gb, SL_T5.index(s))
                    if isinstance(ga, int) and ga < 2:
                        prepare(ga, s)

            def next_batch():
                pe.wait_ge(kv_in, 16)

            prepare_first()
            main_loop(pe, body, PER_BATCH, next_batch)


def rotary_tables():
    inv = (1.0 / np.float32(10000.0) ** (np.arange(0, HD, 2, dtype=np.float32) / np.float32(HD))).astype(np.float32)
    pos = [np.arange(G) + g % PER_BATCH * G for g in range(GROUPS)] + [np.tile(np.arange(S), G // S)]
    ang = np.stack(pos).astype(np.float32)[:, None, :] * np.tile(inv, 4)[None, :, None]
    c, s = np.cos(ang, dtype=np.float32), np.sin(ang, dtype=np.float32)
    return np.ascontiguousarray(np.stack([c, -s, s], axis=2))


def row_masks():
    return np.ascontiguousarray(np.repeat(np.eye(4, dtype=np.float32), HALF, axis=0))


def kernel(x, ctx_1024, g_xattn, g_ffn, L0_xattn_Wq, L0_xattn_Wkv, L0_xattn_Wout, L0_ffn_fast_b, L0_ffn_w_fc,
           L0_ffn_w_proj, L0_ffn_u, L0_ffn_v, L0_ffn_gate, L1_xattn_W, L1_xattn_b, L1_ffn_w1, L1_ffn_b1, L1_ffn_w2,
           L1_ffn_b2):
    import concourse.bacc as bacc
    from concourse.bass_utils import run_bass_kernel_spmd

    a = np.ascontiguousarray
    perm = np.arange(D).reshape(2, 4, 2, HALF).transpose(0, 2, 1, 3).reshape(D)
    wkv = np.asarray(L0_xattn_Wkv)
    arrays = {
        "x": a(np.asarray(x).reshape(GROUPS, G, D)),
        "ctxT": a(np.asarray(ctx_1024).transpose(2, 0, 1).reshape(D, BATCH * S)),
        "gx": a(g_xattn), "gf": a(g_ffn),
        "wqT": a(np.asarray(L0_xattn_Wq)[perm].T),
        "wkvT": a(np.concatenate([wkv[:D][perm], wkv[D:]]).T),
        "woT": a(np.asarray(L0_xattn_Wout).T),
        "fast_b": a(L0_ffn_fast_b), "w_fc": a(L0_ffn_w_fc), "w_proj": a(L0_ffn_w_proj), "uT": a(np.asarray(L0_ffn_u).T),
        "vT": a(np.asarray(L0_ffn_v).T), "gate": a(np.asarray(L0_ffn_gate).reshape(1)),
        "wxT": a(np.asarray(L1_xattn_W)[:, :D].T), "wcT": a(np.asarray(L1_xattn_W)[:, D:].T), "bx": a(L1_xattn_b),
        "w1": a(L1_ffn_w1), "b1": a(L1_ffn_b1), "w2": a(L1_ffn_w2), "b2": a(L1_ffn_b2),
        "rope": rotary_tables(), "mask": row_masks(),
    }
    nc = bacc.Bacc("TRN2", target_bir_lowering=False, num_devices=1)
    args = [nc.dram_tensor(f"in_{n}", v.shape, mybir.dt.from_np(v.dtype), kind="ExternalInput").ap()
            for n, v in arrays.items()]
    args.append(nc.dram_tensor("kv_other", (P, KVSIZE), F16, kind="Internal").ap())
    args.append(nc.dram_tensor("out", (GROUPS, G, D), F32, kind="ExternalOutput").ap())
    build(nc, *args)
    r = run_bass_kernel_spmd(nc, [{f"in_{n}": v for n, v in arrays.items()}], core_ids=[0])
    return r.results[0]["out"].reshape(BATCH, SEQ, D)
```
